# Optimizing a Trainium2 kernel written in Bass

```python
import numpy as np
import jax
import jax.numpy as jnp

def _softmax(x, axis=-1):
    return jax.nn.softmax(x, axis=axis)

def _gelu(x):
    return jax.nn.gelu(x, approximate=True)

def _silu(x):
    return jax.nn.silu(x)

def _sigmoid(x):
    return jax.nn.sigmoid(x)

def _layernorm(x, axis=-1, eps=1e-05):
    m = jnp.mean(x, axis=axis, keepdims=True)
    v = jnp.var(x, axis=axis, keepdims=True)
    return (x - m) / jnp.sqrt(v + eps)

def _scatter_add(tgt, idx, src, axis=0):
    return tgt.at[idx].add(src)

def _segment_sum(src, seg, n):
    return jax.ops.segment_sum(src, seg, n)
kernel_name = 'mk_conv_seq_d2_conv_nchw1024_r2_0e93b4'

def setup_inputs(seed: int=0):
    np.random.seed(seed)
    _w = jnp.asarray

    def _rec_inputs():
        import jax
        import jax.numpy as jnp
        _gk = jax.random.key(seed)
        x = -0.0003929 + 0.9999 * jax.random.normal(jax.random.fold_in(_gk, 1), (16, 512, 32, 32), jnp.float32)
        return x
    x = _rec_inputs()

    def _L0_conv_setup():
        import jax, jax.numpy as jnp
        import numpy as np
        NUM_MODELS = 32
        IN_CHANNELS = 16
        HIDDEN = 64
        B, H, W = (16, 32, 32)

        def _perceive(x):
            b, mc, h, w = x.shape
            padded = jnp.pad(x, ((0, 0), (0, 0), (1, 1), (1, 1)))
            shifts = [x]
            for r in (-1, 0, 1):
                for c in (-1, 0, 1):
                    if r == 0 and c == 0:
                        continue
                    shifts.append(padded[:, :, r + 1:r + 1 + h, c + 1:c + 1 + w])
            return jnp.concatenate(shifts, axis=1)
        key = jax.random.key(seed)
        k1, k2, k3, k4, k5 = jax.random.split(key, 5)
        M, C, Hd = (NUM_MODELS, IN_CHANNELS, HIDDEN)
        x = jax.random.normal(k1, (B, M * C, H, W), dtype=jnp.float32)
        w1 = jax.random.normal(k2, (M, Hd, 9 * C), dtype=jnp.float32) * 0.05
        b1 = jax.random.normal(k3, (M * Hd,), dtype=jnp.float32) * 0.05
        w2 = jax.random.normal(k4, (M, C, Hd), dtype=jnp.float32) * 0.05
        b2 = jax.random.normal(k5, (M * C,), dtype=jnp.float32) * 0.05
        return {'x': x, 'w1': w1, 'b1': b1, 'w2': w2, 'b2': b2}
    _L0_conv_all = _L0_conv_setup()
    _L0_conv_in = {k: v for k, v in _L0_conv_all.items() if k in ('w1', 'b1', 'w2', 'b2')}
    del _L0_conv_all

    def _L1_conv_setup():
        import jax, jax.numpy as jnp
        import numpy as np
        C = 512
        CI = 128
        BN_EPS = 1e-05
        key = jax.random.key(seed)
        ks = jax.random.split(key, 12)
        B, H, W = (16, 32, 32)
        xavier = lambda k, o, i: jax.random.uniform(k, (o, i), jnp.float32, -np.sqrt(6.0 / (o + i)), np.sqrt(6.0 / (o + i)))
        return {'x': jax.random.normal(ks[0], (B, C, H, W), jnp.float32), 'theta_w': xavier(ks[1], CI, C), 'theta_b': jnp.zeros((CI,), jnp.float32), 'phi_w': xavier(ks[2], CI, C), 'phi_b': jnp.zeros((CI,), jnp.float32), 'g_w': xavier(ks[3], CI, C), 'g_b': jnp.zeros((CI,), jnp.float32), 'w_w': xavier(ks[4], C, CI), 'w_b': jnp.zeros((C,), jnp.float32), 'bn_gamma': jax.random.normal(ks[5], (C,), jnp.float32) * 0.1 + 1.0, 'bn_beta': jax.random.normal(ks[6], (C,), jnp.float32) * 0.1, 'bn_mean': jax.random.normal(ks[7], (C,), jnp.float32) * 0.1, 'bn_var': jax.random.uniform(ks[8], (C,), jnp.float32, 0.5, 1.5)}
    _L1_conv_all = _L1_conv_setup()
    _L1_conv_in = {k: v for k, v in _L1_conv_all.items() if k in ('theta_w', 'theta_b', 'phi_w', 'phi_b', 'g_w', 'g_b', 'w_w', 'w_b', 'bn_gamma', 'bn_beta', 'bn_mean', 'bn_var')}
    del _L1_conv_all
    return {'x': x, 'L0_conv_w1': _L0_conv_in['w1'], 'L0_conv_b1': _L0_conv_in['b1'], 'L0_conv_w2': _L0_conv_in['w2'], 'L0_conv_b2': _L0_conv_in['b2'], 'L1_conv_theta_w': _L1_conv_in['theta_w'], 'L1_conv_theta_b': _L1_conv_in['theta_b'], 'L1_conv_phi_w': _L1_conv_in['phi_w'], 'L1_conv_phi_b': _L1_conv_in['phi_b'], 'L1_conv_g_w': _L1_conv_in['g_w'], 'L1_conv_g_b': _L1_conv_in['g_b'], 'L1_conv_w_w': _L1_conv_in['w_w'], 'L1_conv_w_b': _L1_conv_in['w_b'], 'L1_conv_bn_gamma': _L1_conv_in['bn_gamma'], 'L1_conv_bn_beta': _L1_conv_in['bn_beta'], 'L1_conv_bn_mean': _L1_conv_in['bn_mean'], 'L1_conv_bn_var': _L1_conv_in['bn_var']}

def reference(x, L0_conv_w1, L0_conv_b1, L0_conv_w2, L0_conv_b2, L1_conv_theta_w, L1_conv_theta_b, L1_conv_phi_w, L1_conv_phi_b, L1_conv_g_w, L1_conv_g_b, L1_conv_w_w, L1_conv_w_b, L1_conv_bn_gamma, L1_conv_bn_beta, L1_conv_bn_mean, L1_conv_bn_var):
    import jax
    import jax.numpy as jnp

    def _L0_conv_ref(x, w1, b1, w2, b2):
        import jax, jax.numpy as jnp
        import numpy as np
        NUM_MODELS = 32
        IN_CHANNELS = 16
        HIDDEN = 64
        B, H, W = (16, 32, 32)

        def _perceive(x):
            b, mc, h, w = x.shape
            padded = jnp.pad(x, ((0, 0), (0, 0), (1, 1), (1, 1)))
            shifts = [x]
            for r in (-1, 0, 1):
                for c in (-1, 0, 1):
                    if r == 0 and c == 0:
                        continue
                    shifts.append(padded[:, :, r + 1:r + 1 + h, c + 1:c + 1 + w])
            return jnp.concatenate(shifts, axis=1)
        M, C, Hd = (NUM_MODELS, IN_CHANNELS, HIDDEN)
        b, _, h, w = x.shape
        perception = _perceive(x)
        per_g = perception.reshape(b, M, 9 * C, h, w)
        hdn = jnp.einsum('bmchw,mdc->bmdhw', per_g, w1) + b1.reshape(1, M, Hd, 1, 1)
        hdn = jax.nn.relu(hdn)
        dx = jnp.einsum('bmdhw,mcd->bmchw', hdn, w2) + b2.reshape(1, M, C, 1, 1)
        return x + dx.reshape(b, M * C, h, w)

    def _L1_conv_ref(x, theta_w, theta_b, phi_w, phi_b, g_w, g_b, w_w, w_b, bn_gamma, bn_beta, bn_mean, bn_var):
        import jax, jax.numpy as jnp
        import numpy as np
        C = 512
        CI = 128
        BN_EPS = 1e-05
        B, Cc, H, W = x.shape
        N = H * W
        xf = x.reshape(B, Cc, N)
        theta = jnp.einsum('oc,bcn->bno', theta_w, xf) + theta_b
        phi = jnp.einsum('oc,bcn->bon', phi_w, xf) + phi_b[:, None]
        g = jnp.einsum('oc,bcn->bno', g_w, xf) + g_b
        attn = jax.nn.softmax(jnp.einsum('bno,bom->bnm', theta, phi), axis=-1)
        y = jnp.einsum('bnm,bmo->bno', attn, g)
        z = jnp.einsum('co,bno->bcn', w_w, y) + w_b[None, :, None]
        inv = bn_gamma / jnp.sqrt(bn_var + BN_EPS)
        z = (z - bn_mean[None, :, None]) * inv[None, :, None] + bn_beta[None, :, None]
        return z.reshape(B, Cc, H, W) + x

    def _gn(v, G=32, eps=1e-05):
        B_, C_, H_, W_ = v.shape
        g = v.reshape(B_, G, C_ // G, H_, W_)
        m = jnp.mean(g, axis=(2, 3, 4), keepdims=True)
        s = jnp.var(g, axis=(2, 3, 4), keepdims=True)
        return ((g - m) / jnp.sqrt(s + eps)).reshape(v.shape)

    def _ln_c(v, eps=1e-06):
        m = jnp.mean(v, axis=1, keepdims=True)
        s = jnp.var(v, axis=1, keepdims=True)
        return (v - m) / jnp.sqrt(s + eps)

    def _ln_t(v, eps=1e-05):
        m = jnp.mean(v, axis=-1, keepdims=True)
        s = jnp.var(v, axis=-1, keepdims=True)
        return (v - m) / jnp.sqrt(s + eps)

    def _to_tokens(v):
        B_, C_, H_, W_ = v.shape
        return v.reshape(B_, C_, H_ * W_).transpose(0, 2, 1)

    def _from_tokens(t, like):
        B_, C_, H_, W_ = like.shape
        return t.transpose(0, 2, 1).reshape(B_, C_, H_, W_)
    x = _L0_conv_ref(x, L0_conv_w1, L0_conv_b1, L0_conv_w2, L0_conv_b2)
    x = _L1_conv_ref(x, L1_conv_theta_w, L1_conv_theta_b, L1_conv_phi_w, L1_conv_phi_b, L1_conv_g_w, L1_conv_g_b, L1_conv_w_w, L1_conv_w_b, L1_conv_bn_gamma, L1_conv_bn_beta, L1_conv_bn_mean, L1_conv_bn_var)
    return x

_drawn_inputs = setup_inputs


def setup_inputs(seed=0):
    import zlib

    import numpy as np

    out = dict(_drawn_inputs(seed))
    spreads = {'L1_conv_theta_b': (0.0, 0.1),
     'L1_conv_phi_b': (0.0, 0.1),
     'L1_conv_g_b': (0.0, 0.1),
     'L1_conv_w_b': (0.0, 0.1)}
    factors = {}
    for name, (base, spread) in spreads.items():
        noise = np.random.default_rng([zlib.crc32(name.encode()), seed]).standard_normal(out[name].shape)
        drawn = base * np.exp(spread * noise) if base else spread * noise
        out[name] = jnp.asarray(drawn.astype(out[name].dtype))
    for name, factor in factors.items():
        out[name] = (out[name] * factor).astype(out[name].dtype)
    return out
```

```python
import concourse.bass as bass
from concourse import mybir
from contextlib import ExitStack

F32 = mybir.dt.float32
F32R = mybir.dt.float32r
ALU = mybir.AluOpType
ACT = mybir.ActivationFunctionType
AX = mybir.AxisListType

P = 128
BATCH, CHANNELS, SIDE = 16, 512, 32
PIXELS = SIDE * SIDE
PITCH = SIDE + 2
PADDED = PITCH * PITCH
BLOCKS = CHANNELS // P
HALF = PIXELS // 2
HALF_ROWS = SIDE // 2
HIDDEN, MODEL_CH, WINDOW = 64, 16, 144
MODELS = 32
GROUPS = BLOCKS
PAIRS = 4
SLOTS = 2 * GROUPS
GROUP_CHUNKS = 9
SHIFTS = [(0, 0)] + [(r, c) for r in (-1, 0, 1) for c in (-1, 0, 1) if (r, c) != (0, 0)]
QBLOCKS = PIXELS // P
QUARTER = 2 * P
QUARTERS = PIXELS // QUARTER
BN_EPS = 1e-5


def conv_attention(nc, x, w1_rows, w2_t, proj_t, ww, per_channel, out):
    with ExitStack() as ctx:
        def sb(name, shape, dt=F32):
            return ctx.enter_context(nc.sbuf_tensor(name, shape, dt))

        def sem(name):
            return ctx.enter_context(nc.semaphore(name))

        xp = sb("xp", [P, BLOCKS, PADDED])
        xp_hi = sb("xp_hi", [P, BLOCKS, PADDED], F32R)
        xp_lo = sb("xp_lo", [P, BLOCKS, PADDED], F32R)
        x1 = sb("x1", [P, BLOCKS, PIXELS])
        x1_hi = sb("x1_hi", [P, BLOCKS, PIXELS], F32R)
        x1_lo = sb("x1_lo", [P, BLOCKS, PIXELS], F32R)
        hidden = sb("hidden", [P, PAIRS, HALF])
        w_first = sb("w_first", [P, GROUPS, PAIRS, HIDDEN])
        w_last = sb("w_last", [P, GROUPS, PAIRS, HIDDEN])
        w_mid_hi = sb("w_mid_hi", [P, GROUPS, PAIRS, P], F32R)
        w_mid_lo = sb("w_mid_lo", [P, GROUPS, PAIRS, P], F32R)
        w2s = sb("w2s", [P, GROUPS * PAIRS, 2 * MODEL_CH])
        wp_hi = sb("wp_hi", [P, 3, BLOCKS, P], F32R)
        wp_lo = sb("wp_lo", [P, 3, BLOCKS, P], F32R)
        ww_hi = sb("ww_hi", [P, CHANNELS], F32R)
        ww_lo = sb("ww_lo", [P, CHANNELS], F32R)
        tp_hi = sb("tp_hi", [P, 2, PIXELS], F32R)
        tp_lo = sb("tp_lo", [P, 2, PIXELS], F32R)
        g_hi = sb("g_hi", [P, QBLOCKS, P], F32R)
        g_lo = sb("g_lo", [P, QBLOCKS, P], F32R)
        probs = sb("probs", [P, 2, PIXELS])
        pt_hi = sb("pt_hi", [P, QBLOCKS, QUARTER], F32R)
        pt_lo = sb("pt_lo", [P, QBLOCKS, QUARTER], F32R)
        y_hi = sb("y_hi", [P, QUARTER], F32R)
        y_lo = sb("y_lo", [P, QUARTER], F32R)
        ident = sb("ident", [P, P])
        columns = sb("columns", [P, per_channel.shape[1]])
        b1s, b2s, pbs = columns[:, 0:16], columns[:, 16:20], columns[:, 20:23]
        bn = columns[:, 23:43].rearrange("p (v k) -> p v k", v=5)
        inv = sb("inv", [P, BLOCKS])
        shift = sb("shift", [P, BLOCKS])
        bn_a = sb("bn_a", [P, BLOCKS])
        bn_b = sb("bn_b", [P, BLOCKS])
        neg_max = sb("neg_max", [P, 2])
        row_sum = sb("row_sum", [P, 2])
        row_inv = sb("row_inv", [P, 2])

        stage = hidden[:, :, :].rearrange("p q n -> p (q n)").rearrange("p (s n) -> p s n", s=2)
        g_t = probs[:, 0, :]
        mid_raw = x1[:, 0:2, :].rearrange("p k n -> p (k n)").rearrange("p (g q m) -> p g q m", g=GROUPS, q=PAIRS)
        ww_raw = x1[:, 3, 0:BLOCKS * P].rearrange("p (k o) -> p k o", k=BLOCKS)
        wp_raw = probs[:, :, :].rearrange("p a n -> p (a n)")[:, 0:3 * BLOCKS * P].rearrange(
            "p (w k o) -> p w k o", w=3, k=BLOCKS)

        ps = ctx.enter_context(nc.psum_tensor("ps", [P, 8, HALF], F32))
        BANK_T, BANK_Y, BANK_Z = 4, 6, 7
        score_banks = [ps[:, 0:2, :], ps[:, 2:4, :]]

        def padded(t, k):
            return t[:, k, :].rearrange("p (h w) -> p h w", w=PITCH)

        def shifted(t, chunk, half):
            dr, dc = SHIFTS[chunk // BLOCKS]
            r0 = 1 + dr + HALF_ROWS * half
            return padded(t, chunk % BLOCKS)[:, r0:r0 + HALF_ROWS, 1 + dc:1 + dc + SIDE]

        def inside(t, k):
            return padded(t, k)[:, 1:1 + SIDE, 1:1 + SIDE]

        w_mid_loaded = sem("w_mid_loaded")
        w_l0_loaded = sem("w_l0_loaded")
        w_l1_loaded = sem("w_l1_loaded")
        borders_zero = sem("borders_zero")
        weights_zero = sem("weights_zero")
        ident_zero = sem("ident_zero")
        ident_ready = sem("ident_ready")
        w_mid_rounded = sem("w_mid_rounded")
        w_mid_split = sem("w_mid_split")
        wp_rounded = sem("wp_rounded")
        wp_split = sem("wp_split")
        bn_step = sem("bn_step")
        var_ready = sem("var_ready")
        std_ready = sem("std_ready")
        ww_scaled = sem("ww_scaled")
        ww_transposed = sem("ww_transposed")
        ww_rounded = sem("ww_rounded")
        ww_split = sem("ww_split")

        x_loaded = [sem("x_loaded_0"), sem("x_loaded_1")]
        xp_copied = sem("xp_copied")
        xp_rounded = sem("xp_rounded")
        xp_split = sem("xp_split")
        hidden_summed = sem("hidden_summed")
        hidden_ready = sem("hidden_ready")
        dx_summed = sem("dx_summed")
        x1_ready = sem("x1_ready")
        x1_rounded = sem("x1_rounded")
        x1_split = sem("x1_split")
        projected = sem("projected")
        proj_biased = sem("proj_biased")
        tp_split = sem("tp_split")
        scored = sem("scored")
        max_found = sem("max_found")
        exp_done = sem("exp_done")
        inv_done = sem("inv_done")
        normalized = sem("normalized")
        transposed = sem("transposed")
        t_rounded = sem("t_rounded")
        t_split = sem("t_split")
        y_summed = sem("y_summed")
        y_rounded = sem("y_rounded")
        y_split = sem("y_split")
        z_summed = sem("z_summed")
        out_added = sem("out_added")
        stored = [sem("stored_0"), sem("stored_1")]

        TH, PH, G = 0, 1, 2
        T_PER = 2 * (QBLOCKS + 1)

        block = ctx.enter_context(nc.Block())

        @block.sync
        def _(sp):
            def load_x(n, k):
                if k >= 2:
                    sp.wait_ge(xp_copied, n * BLOCKS + k - 1)
                sp.dma_start(stage[:, k % 2, :], x[n, k * P:(k + 1) * P, :]).then_inc(x_loaded[k % 2], 16)

            def store_quarter(n, j):
                sp.wait_ge(out_added, n * 8 + 2 * j + 2)
                sp.dma_start(out[n, :, j * QUARTER:(j + 1) * QUARTER].rearrange("(k p) n -> p k n", p=P),
                             x1[:, :, j * QUARTER:(j + 1) * QUARTER]).then_inc(stored[j // 2], 16)

            def batch(n, has_next):
                if has_next:
                    sp.wait_ge(dx_summed, n * SLOTS + SLOTS)
                    for k in range(BLOCKS):
                        load_x(n + 1, k)
                for j in range(QUARTERS):
                    store_quarter(n, j)

            load_x(0, 0)
            load_x(0, 1)
            rows = w1_rows.rearrange("(g r) d -> r g d", g=GROUPS)
            sp.wait_ge(weights_zero, 1)
            for q in range(PAIRS):
                at, cut = 2 * P * q, 32 * q + 16
                sp.dma_start(mid_raw[0:cut, :, q, 0:HIDDEN], rows[at + P:at + P + cut]).then_inc(w_mid_loaded, 16)
                sp.dma_start(mid_raw[cut:P, :, q, HIDDEN:P], rows[at + P + cut:at + 2 * P]).then_inc(w_mid_loaded, 16)
            load_x(0, 2)
            load_x(0, 3)
            for q in range(PAIRS):
                at = 2 * P * q
                sp.dma_start(w_first[32 * q:P, :, q, :], rows[at + 32 * q:at + P]).then_inc(w_l0_loaded, 16)
                sp.dma_start(w_last[0:32 * q + 32, :, q, :],
                             rows[at + 2 * P:at + 2 * P + 32 * q + 32]).then_inc(w_l0_loaded, 16)
            for half in range(2):
                sp.dma_start(w2s[half * HIDDEN:(half + 1) * HIDDEN, :, half * MODEL_CH:(half + 1) * MODEL_CH],
                             w2_t[half].rearrange("m d c -> d m c")).then_inc(w_l0_loaded, 16)
            sp.dma_start(columns[:, :], per_channel).then_inc(w_l0_loaded, 16)
            for w in range(3):
                sp.dma_start(wp_raw[:, w, :, :], proj_t[w].rearrange("(k p) o -> p k o", p=P)).then_inc(w_l1_loaded, 16)
            sp.dma_start(ww_raw, ww.rearrange("(k p) o -> p k o", p=P)).then_inc(w_l1_loaded, 16)

            with sp.Fori(0, BATCH - 1) as n:
                batch(n, True)
            batch(BATCH - 1, False)
            for s in stored:
                sp.wait_ge(s, 16 * 2 * BATCH)

        W_MID_DMAS, W_L0_DMAS, W_L1_DMAS = 2 * PAIRS, 2 * PAIRS + 3, 4

        @block.tensor
        def _(pe):
            mm = nc.tensor.matmul

            def hidden_pair(n, s, q):
                half, grp = divmod(s, GROUPS)
                bank, first = ps[:, q % 2, :], GROUP_CHUNKS * grp + 2 * q
                k = s * PAIRS + q
                if k >= 2:
                    pe.wait_ge(hidden_ready, n * SLOTS * PAIRS + k - 1)
                if k == 0:
                    pe.wait_ge(xp_rounded, n * BLOCKS + BLOCKS)
                    pe.wait_ge(xp_split, n * BLOCKS + BLOCKS)
                mid_hi, mid_lo = w_mid_hi[:, grp, q, :], w_mid_lo[:, grp, q, :]
                mm(bank, mid_hi, shifted(xp_hi, first + 1, half), start=True, stop=False, skip_group_check=True)
                mm(bank, mid_hi, shifted(xp_lo, first + 1, half), start=False, stop=False, skip_group_check=True)
                mm(bank, mid_lo, shifted(xp_hi, first + 1, half), start=False, stop=False, skip_group_check=True)
                mm(bank[0:HIDDEN], w_first[:, grp, q, :], shifted(xp, first, half), start=False, stop=True,
                   skip_group_check=True)
                mm(bank[HIDDEN:P], w_last[:, grp, q, :], shifted(xp, first + 2, half), start=False, stop=True,
                   skip_group_check=True).then_inc(hidden_summed, 1)

            def dx(n, s):
                pe.wait_ge(hidden_ready, n * SLOTS * PAIRS + (s + 1) * PAIRS)
                if s > 0:
                    pe.wait_ge(x1_ready, n * SLOTS + s)
                for q in range(PAIRS):
                    last = mm(ps[32 * q:32 * q + 32, BANK_Z, :], w2s[:, (s % GROUPS) * PAIRS + q, :],
                              hidden[:, q, :], start=True, stop=True)
                last.then_inc(dx_summed, 1)

            def project(n, half, w):
                bank = ps[:, BANK_T + (half * 3 + w) % 2, :]
                if w == TH:
                    pe.wait_ge(x1_split, n * SLOTS + GROUPS * (half + 1))
                step = half * 3 + w
                if step == 2 or step == 3:
                    pe.wait_ge(tp_split, n * 4 + step - 1)
                elif step == 4:
                    pe.wait_ge(proj_biased, n * 6 + 3)
                elif step == 5:
                    pe.wait_ge(tp_split, n * 4 + 3)
                cols = slice(half * HALF, (half + 1) * HALF)
                for k in range(BLOCKS):
                    mm(bank, wp_hi[:, w, k, :], x1_hi[:, k, cols], start=(k == 0), stop=False)
                    mm(bank, wp_hi[:, w, k, :], x1_lo[:, k, cols], start=False, stop=False)
                    last = mm(bank, wp_lo[:, w, k, :], x1_hi[:, k, cols], start=False, stop=(k == BLOCKS - 1))
                last.then_inc(projected, 1)

            def scores(n, i):
                if i == 0:
                    pe.wait_ge(tp_split, n * 4 + 4)
                if i >= 2:
                    pe.wait_ge(exp_done, n * QBLOCKS + i - 1)
                rows = slice(i * P, (i + 1) * P)
                for half in range(2):
                    bank, cols = ps[:, 2 * (i % 2) + half, :], slice(half * HALF, (half + 1) * HALF)
                    mm(bank, tp_hi[:, TH, rows], tp_hi[:, PH, cols], start=True, stop=False)
                    mm(bank, tp_hi[:, TH, rows], tp_lo[:, PH, cols], start=False, stop=False)
                    last = mm(bank, tp_lo[:, TH, rows], tp_hi[:, PH, cols], start=False, stop=True)
                last.then_inc(scored, 1)

            def transpose(n, tau):
                for u in range(2):
                    if tau == 0:
                        pe.wait_ge(proj_biased, n * 6 + 6)
                        src = g_t
                        if u == 0:
                            pe.wait_ge(tp_split, n * 4 + 4)
                    else:
                        if u == 0:
                            pe.wait_ge(normalized, n * QBLOCKS + tau)
                        pe.wait_ge(t_split, n * T_PER + 2 * (tau - 1) + u + 1)
                        src = probs[:, (tau - 1) % 2, :]
                    for v in range(4):
                        c = (4 * u + v) * P
                        last = nc.tensor.transpose(ps[:, BANK_T + u, v * P:(v + 1) * P], src[:, c:c + P], ident[:, :])
                    last.then_inc(transposed, 1)

            def attend(n, j):
                pe.wait_ge(t_split, n * T_PER + 2 * (2 * j + 3))
                if j > 0:
                    pe.wait_ge(y_split, n * QUARTERS + j)
                bank = ps[:, BANK_Y, 0:QUARTER]
                for m in range(QBLOCKS):
                    mm(bank, g_hi[:, m, :], pt_hi[:, m, :], start=(m == 0), stop=False)
                    mm(bank, g_hi[:, m, :], pt_lo[:, m, :], start=False, stop=False)
                    last = mm(bank, g_lo[:, m, :], pt_hi[:, m, :], start=False, stop=(m == QBLOCKS - 1))
                last.then_inc(y_summed, 1)

            def output(n, j, v):
                if v == 0:
                    pe.wait_ge(y_split, n * QUARTERS + j + 1)
                if j > 0 or v > 0:
                    pe.wait_ge(out_added, n * 8 + 2 * j + v)
                for e in range(2):
                    c = slice((2 * v + e) * P, (2 * v + e + 1) * P)
                    bank = ps[:, BANK_Z, e * QUARTER:(e + 1) * QUARTER]
                    mm(bank, ww_hi[:, c], y_hi[:, :], start=True, stop=False)
                    mm(bank, ww_hi[:, c], y_lo[:, :], start=False, stop=False)
                    last = mm(bank, ww_lo[:, c], y_hi[:, :], start=False, stop=True)
                last.then_inc(z_summed, 1)

            def image_slots(n, first_slot):
                for s in range(first_slot, SLOTS):
                    hidden_pair(n, s, 0)
                    dx(n, s - 1)
                    for q in range(1, PAIRS):
                        hidden_pair(n, s, q)

            def batch(n, has_next):
                project(n, 0, TH)
                dx(n, SLOTS - 1)
                project(n, 0, PH)
                project(n, 0, G)
                for w in (TH, PH, G):
                    project(n, 1, w)
                scores(n, 0)
                transpose(n, 0)
                scores(n, 1)
                for i in range(QBLOCKS):
                    j = i // 2
                    if i % 2 == 0:
                        if i + 2 < QBLOCKS:
                            scores(n, i + 2)
                        if j > 0:
                            attend(n, j - 1)
                        transpose(n, i + 1)
                        if i == QBLOCKS - 2 and has_next:
                            hidden_pair(n + 1, 0, 0)
                    else:
                        if j > 0:
                            output(n, j - 1, 0)
                        if i + 2 < QBLOCKS:
                            scores(n, i + 2)
                        transpose(n, i + 1)
                        if j > 0:
                            output(n, j - 1, 1)
                if has_next:
                    hidden_pair(n + 1, 0, 1)
                    hidden_pair(n + 1, 0, 2)
                attend(n, QUARTERS - 1)
                if has_next:
                    hidden_pair(n + 1, 0, 3)
                output(n, QUARTERS - 1, 0)
                output(n, QUARTERS - 1, 1)
                if has_next:
                    pe.wait_ge(out_added, n * 8 + 8)
                    image_slots(n + 1, 1)

            pe.wait_ge(ident_ready, 1)
            pe.wait_ge(w_mid_split, 1)
            pe.wait_ge(w_l0_loaded, 16 * W_L0_DMAS)
            for q in range(PAIRS):
                hidden_pair(0, 0, q)
            pe.wait_ge(ww_scaled, BLOCKS)
            for k in range(BLOCKS):
                last = nc.tensor.transpose(ps[:, BANK_T, k * P:(k + 1) * P], ww_raw[:, k, :], ident[:, :])
            last.then_inc(ww_transposed, 1)
            image_slots(0, 1)
            pe.wait_ge(wp_split, 1)
            pe.wait_ge(ww_split, 1)
            with pe.Fori(0, BATCH - 1) as n:
                batch(n, True)
            batch(BATCH - 1, False)

        @block.scalar
        def _(act):
            activation = nc.scalar.activation

            def relu(n, s, q):
                act.wait_ge(hidden_summed, n * SLOTS * PAIRS + s * PAIRS + q + 1)
                if q == 0 and s > 0:
                    act.wait_ge(dx_summed, n * SLOTS + s)
                grp = s % GROUPS
                activation(hidden[:, q, :], ps[:, q % 2, :], ACT.Relu,
                           bias=b1s[:, grp * PAIRS + q:grp * PAIRS + q + 1]).then_inc(hidden_ready, 1)

            def round_x1(n, s):
                half, grp = divmod(s, GROUPS)
                act.wait_ge(x1_ready, n * SLOTS + s + 1)
                cols = slice(half * HALF, (half + 1) * HALF)
                nc.scalar.copy(x1_hi[:, grp, cols], x1[:, grp, cols]).then_inc(x1_rounded, 1)

            def bias_projection(n, half, w):
                step = half * 3 + w
                act.wait_ge(projected, n * 6 + step + 1)
                cols = slice(half * HALF, (half + 1) * HALF)
                dst = g_t[:, cols] if w == G else tp_hi[:, w, cols]
                activation(dst, ps[:, BANK_T + step % 2, :], ACT.Identity,
                           bias=pbs[:, w:w + 1]).then_inc(proj_biased, 1)

            def exp_rows(n, i):
                act.wait_ge(max_found, n * QBLOCKS + i + 1)
                if i == 0:
                    act.wait_ge(transposed, n * T_PER + 2)
                elif i >= 2:
                    act.wait_ge(transposed, n * T_PER + 2 * i)
                activation(probs[:, i % 2, :], score_banks[i % 2], ACT.Exp, bias=neg_max[:, i % 2:i % 2 + 1],
                           accum_out=row_sum[:, i % 2:i % 2 + 1]).then_inc(exp_done, 1)

            def round_transposed(n, tau):
                for u in range(2):
                    act.wait_ge(transposed, n * T_PER + 2 * tau + u + 1)
                    src = ps[:, BANK_T + u, :].rearrange("p (m n) -> p m n", m=4)
                    if tau == 0:
                        dst = g_hi[:, 4 * u:4 * u + 4, :]
                    else:
                        if u == 0 and tau >= 3 and tau % 2 == 1:
                            act.wait_ge(y_summed, n * QUARTERS + (tau - 1) // 2)
                        c = (tau - 1) % 2 * P
                        dst = pt_hi[:, 4 * u:4 * u + 4, c:c + P]
                    nc.scalar.copy(dst, src).then_inc(t_rounded, 1)

            def round_y(n, j):
                act.wait_ge(y_summed, n * QUARTERS + j + 1)
                if j > 0:
                    act.wait_ge(z_summed, n * 8 + 2 * j)
                nc.scalar.copy(y_hi[:, :], ps[:, BANK_Y, 0:QUARTER]).then_inc(y_rounded, 1)

            def round_image(n, k):
                act.wait_ge(xp_copied, n * BLOCKS + k + 1)
                nc.scalar.copy(xp_hi[:, k, :], xp[:, k, :]).then_inc(xp_rounded, 1)

            def image_slots(n, first_slot):
                for s in range(first_slot, SLOTS):
                    relu(n, s, 0)
                    relu(n, s, 1)
                    round_x1(n, s - 1)
                    relu(n, s, 2)
                    relu(n, s, 3)

            def batch(n, has_next):
                bias_projection(n, 0, TH)
                round_x1(n, SLOTS - 1)
                bias_projection(n, 0, PH)
                bias_projection(n, 0, G)
                if has_next:
                    round_image(n + 1, 0)
                for w in (TH, PH, G):
                    bias_projection(n, 1, w)
                if has_next:
                    round_image(n + 1, 1)
                round_transposed(n, 0)
                exp_rows(n, 0)
                exp_rows(n, 1)
                for i in range(QBLOCKS):
                    j = i // 2
                    if i % 2 == 0 and j > 0:
                        round_y(n, j - 1)
                    round_transposed(n, i + 1)
                    if i + 2 < QBLOCKS:
                        exp_rows(n, i + 2)
                    if has_next and i in (2, 4):
                        round_image(n + 1, 1 + i // 2)
                    if has_next and i == QBLOCKS - 2:
                        relu(n + 1, 0, 0)
                if has_next:
                    relu(n + 1, 0, 1)
                    relu(n + 1, 0, 2)
                round_y(n, QUARTERS - 1)
                if has_next:
                    relu(n + 1, 0, 3)
                    image_slots(n + 1, 1)

            act.wait_ge(w_mid_loaded, 16 * W_MID_DMAS)
            nc.scalar.copy(w_mid_hi[:, :, :, :], mid_raw).then_inc(w_mid_rounded, 1)
            for k in range(BLOCKS):
                round_image(0, k)
            act.wait_ge(w_l1_loaded, 16 * W_L1_DMAS)
            nc.scalar.copy(wp_hi[:, :, :, :], wp_raw).then_inc(wp_rounded, 1)
            act.wait_ge(w_l0_loaded, 16 * W_L0_DMAS)
            for q in range(PAIRS):
                relu(0, 0, q)
            act.wait_ge(var_ready, 1)
            nc.scalar.sqrt(bn_b[:, :], bn_a[:, :]).then_inc(std_ready, 1)
            act.wait_ge(ww_transposed, 1)
            nc.scalar.copy(ww_hi[:, :], ps[:, BANK_T, :]).then_inc(ww_rounded, 1)
            image_slots(0, 1)
            with act.Fori(0, BATCH - 1) as n:
                batch(n, True)
            batch(BATCH - 1, False)

        @block.vector
        def _(dve):
            stt = nc.vector.scalar_tensor_tensor

            def sum_x1(n, s):
                half, grp = divmod(s, GROUPS)
                dve.wait_ge(dx_summed, n * SLOTS + s + 1)
                image = inside(xp, grp)[:, half * HALF_ROWS:(half + 1) * HALF_ROWS, :]
                stt(out=x1[:, grp, half * HALF:(half + 1) * HALF].rearrange("p (h w) -> p h w", w=SIDE),
                    in0=ps[:, BANK_Z, :].rearrange("p (h w) -> p h w", w=SIDE), scalar=b2s[:, grp:grp + 1],
                    in1=image, op0=ALU.add, op1=ALU.add).then_inc(x1_ready, 1)

            def split_projection(n, half, w):
                step = half * 3 + w
                dve.wait_ge(proj_biased, n * 6 + step + 1)
                cols = slice(half * HALF, (half + 1) * HALF)
                stt(out=tp_lo[:, w, cols], in0=ps[:, BANK_T + step % 2, :], scalar=pbs[:, w:w + 1],
                    in1=tp_hi[:, w, cols].bitcast(F32), op0=ALU.add, op1=ALU.subtract).then_inc(tp_split, 1)

            def copy_image(n, k):
                dve.wait_ge(x_loaded[k % 2], (n * 2 + k // 2 + 1) * 16)
                nc.vector.tensor_copy(inside(xp, k), stage[:, k % 2, :].rearrange("p (h w) -> p h w", w=SIDE)
                                      ).then_inc(xp_copied, 1)

            def find_max(n, i):
                dve.wait_ge(scored, n * QBLOCKS + i + 1)
                nc.vector.tensor_reduce(neg_max[:, i % 2:i % 2 + 1], score_banks[i % 2], op=ALU.max, axis=AX.XY,
                                        negate=True).then_inc(max_found, 1)

            def normalize(n, i):
                e = slice(i % 2, i % 2 + 1)
                dve.wait_ge(exp_done, n * QBLOCKS + i + 1)
                nc.vector.reciprocal(row_inv[:, e], row_sum[:, e]).then_inc(inv_done, 1)
                dve.wait_ge(inv_done, n * QBLOCKS + i + 1)
                nc.vector.tensor_scalar(probs[:, i % 2, :], probs[:, i % 2, :], row_inv[:, e], None,
                                        ALU.mult).then_inc(normalized, 1)

            def split_transposed(n, tau):
                for u in range(2):
                    dve.wait_ge(t_rounded, n * T_PER + 2 * tau + u + 1)
                    src = ps[:, BANK_T + u, :].rearrange("p (m n) -> p m n", m=4)
                    if tau == 0:
                        hi, lo = (t[:, 4 * u:4 * u + 4, :] for t in (g_hi, g_lo))
                    else:
                        c = (tau - 1) % 2 * P
                        hi, lo = (t[:, 4 * u:4 * u + 4, c:c + P] for t in (pt_hi, pt_lo))
                    nc.vector.tensor_tensor(lo, src, hi.bitcast(F32), ALU.subtract).then_inc(t_split, 1)

            def split_y(n, j):
                dve.wait_ge(y_rounded, n * QUARTERS + j + 1)
                nc.vector.tensor_tensor(y_lo[:, :], ps[:, BANK_Y, 0:QUARTER], y_hi[:, :].bitcast(F32),
                                        ALU.subtract).then_inc(y_split, 1)

            def add_out(n, j, v):
                dve.wait_ge(z_summed, n * 8 + 2 * j + v + 1)
                for e in range(2):
                    k = 2 * v + e
                    place = x1[:, k, j * QUARTER:(j + 1) * QUARTER]
                    last = stt(out=place, in0=ps[:, BANK_Z, e * QUARTER:(e + 1) * QUARTER],
                               scalar=shift[:, k:k + 1], in1=place, op0=ALU.add, op1=ALU.add)
                last.then_inc(out_added, 1)

            def batch(n, has_next):
                split_projection(n, 0, TH)
                sum_x1(n, SLOTS - 1)
                split_projection(n, 0, PH)
                if has_next:
                    dve.wait_ge(hidden_summed, (n + 1) * SLOTS * PAIRS)
                    copy_image(n + 1, 0)
                split_projection(n, 1, TH)
                split_projection(n, 1, PH)
                if has_next:
                    copy_image(n + 1, 1)
                find_max(n, 0)
                split_transposed(n, 0)
                find_max(n, 1)
                normalize(n, 0)
                for i in range(QBLOCKS):
                    j = i // 2
                    if i + 1 < QBLOCKS:
                        normalize(n, i + 1)
                    if i % 2 == 1 and j > 0:
                        add_out(n, j - 1, 0)
                    if i + 2 < QBLOCKS:
                        find_max(n, i + 2)
                    if i % 2 == 0 and j > 0:
                        split_y(n, j - 1)
                    split_transposed(n, i + 1)
                    if i % 2 == 1 and j > 0:
                        add_out(n, j - 1, 1)
                    if has_next and i in (1, 3):
                        copy_image(n + 1, 2 + i // 2)
                split_y(n, QUARTERS - 1)
                add_out(n, QUARTERS - 1, 0)
                add_out(n, QUARTERS - 1, 1)
                if has_next:
                    dve.wait_ge(stored[0], (n + 1) * 32)
                    for s in range(GROUPS):
                        sum_x1(n + 1, s)
                    dve.wait_ge(stored[1], (n + 1) * 32)
                    for s in range(GROUPS, SLOTS - 1):
                        sum_x1(n + 1, s)

            nc.vector.memset(mid_raw, 0.0)
            nc.vector.memset(w_first[:, :, :, :], 0.0)
            nc.vector.memset(w_last[:, :, :, :], 0.0)
            nc.vector.memset(w2s[:, :, :], 0.0).then_inc(weights_zero, 1)
            dve.wait_ge(borders_zero, 1)
            copy_image(0, 0)
            copy_image(0, 1)
            dve.wait_ge(w_mid_rounded, 1)
            nc.vector.tensor_tensor(w_mid_lo[:, :, :, :], mid_raw, w_mid_hi[:, :, :, :].bitcast(F32),
                                    ALU.subtract).then_inc(w_mid_split, 1)
            copy_image(0, 2)
            copy_image(0, 3)
            dve.wait_ge(wp_rounded, 1)
            nc.vector.tensor_tensor(wp_lo[:, :, :, :], wp_raw, wp_hi[:, :, :, :].bitcast(F32),
                                    ALU.subtract).then_inc(wp_split, 1)

            steps = [0]

            def chain(instruction):
                steps[0] += 1
                instruction.then_inc(bn_step, 1)
                dve.wait_ge(bn_step, steps[0])

            WB, GAMMA, BETA, MEAN, VAR = range(5)
            tt, ts = nc.vector.tensor_tensor, nc.vector.tensor_scalar
            dve.wait_ge(w_l0_loaded, 16 * W_L0_DMAS)
            dve.wait_ge(w_l1_loaded, 16 * W_L1_DMAS)
            ts(bn_a[:, :], bn[:, VAR, :], BN_EPS, None, ALU.add).then_inc(var_ready, 1)
            dve.wait_ge(std_ready, 1)
            chain(nc.vector.reciprocal(inv[:, :], bn_b[:, :]))
            chain(tt(bn_b[:, :], inv[:, :], inv[:, :], ALU.mult))
            chain(tt(bn_b[:, :], bn_b[:, :], bn_a[:, :], ALU.mult))
            chain(ts(bn_b[:, :], bn_b[:, :], -0.5, 1.5, ALU.mult, ALU.add))
            chain(tt(inv[:, :], inv[:, :], bn_b[:, :], ALU.mult))
            chain(tt(inv[:, :], inv[:, :], bn[:, GAMMA, :], ALU.mult))
            chain(tt(shift[:, :], bn[:, WB, :], bn[:, MEAN, :], ALU.subtract))
            chain(tt(shift[:, :], shift[:, :], inv[:, :], ALU.mult))
            chain(tt(shift[:, :], shift[:, :], bn[:, BETA, :], ALU.add))
            for k in range(BLOCKS):
                ts(ww_raw[:, k, :], ww_raw[:, k, :], inv[:, k:k + 1], None, ALU.mult).then_inc(ww_scaled, 1)
            dve.wait_ge(ww_rounded, 1)
            tt(ww_lo[:, :], ps[:, BANK_T, :], ww_hi[:, :].bitcast(F32), ALU.subtract).then_inc(ww_split, 1)
            for s in range(SLOTS - 1):
                sum_x1(0, s)
            with dve.Fori(0, BATCH - 1) as n:
                batch(n, True)
            batch(BATCH - 1, False)

        @block.gpsimd
        def _(pool):
            def split_x1(n, s):
                half, grp = divmod(s, GROUPS)
                cols = slice(half * HALF, (half + 1) * HALF)
                pool.wait_ge(x1_rounded, n * SLOTS + s + 1)
                nc.gpsimd.tensor_tensor(x1_lo[:, grp, cols], x1[:, grp, cols], x1_hi[:, grp, cols].bitcast(F32),
                                        ALU.subtract).then_inc(x1_split, 1)

            def split_image(n, k):
                pool.wait_ge(xp_rounded, n * BLOCKS + k + 1)
                nc.gpsimd.tensor_tensor(xp_lo[:, k, :], xp[:, k, :], xp_hi[:, k, :].bitcast(F32),
                                        ALU.subtract).then_inc(xp_split, 1)

            def batch(n, has_next):
                split_x1(n, SLOTS - 1)
                if has_next:
                    for k in range(BLOCKS):
                        split_image(n + 1, k)
                    for s in range(SLOTS - 1):
                        split_x1(n + 1, s)

            nc.gpsimd.memset(xp[:, :, :], 0.0).then_inc(borders_zero, 1)
            nc.gpsimd.memset(ident[:, :], 0.0).then_inc(ident_zero, 1)
            pool.wait_ge(ident_zero, 1)
            nc.gpsimd.affine_select(out=ident[:, :], in_=ident[:, :], compare_op=ALU.not_equal, fill=1.0, base=0,
                                    pattern=[[-1, P]], channel_multiplier=1).then_inc(ident_ready, 1)
            for k in range(BLOCKS):
                split_image(0, k)
            for s in range(SLOTS - 1):
                split_x1(0, s)
            with pool.Fori(0, BATCH - 1) as n:
                batch(n, True)
            batch(BATCH - 1, False)


def kernel(x, L0_conv_w1, L0_conv_b1, L0_conv_w2, L0_conv_b2, L1_conv_theta_w, L1_conv_theta_b, L1_conv_phi_w,
           L1_conv_phi_b, L1_conv_g_w, L1_conv_g_b, L1_conv_w_w, L1_conv_w_b, L1_conv_bn_gamma, L1_conv_bn_beta,
           L1_conv_bn_mean, L1_conv_bn_var):
    import numpy as np
    import concourse.bacc as bacc
    from concourse.bass_utils import run_bass_kernel_spmd

    x = np.asarray(x)
    arrays = {
        "x": x.reshape(BATCH, CHANNELS, PIXELS),
        "w1_rows": np.asarray(L0_conv_w1).transpose(0, 2, 1).reshape(MODELS * WINDOW, HIDDEN),
        "w2_t": np.asarray(L0_conv_w2).transpose(0, 2, 1).reshape(MODELS // 2, 2, HIDDEN, MODEL_CH).transpose(1, 0, 2, 3),
        "proj_t": np.stack([np.asarray(w).T for w in (L1_conv_theta_w, L1_conv_phi_w, L1_conv_g_w)]),
        "ww": np.asarray(L1_conv_w_w),
        "per_channel": np.concatenate([np.asarray(v).reshape(-1, P) for v in (
            L0_conv_b1, L0_conv_b2, L1_conv_theta_b, L1_conv_phi_b, L1_conv_g_b, L1_conv_w_b, L1_conv_bn_gamma,
            L1_conv_bn_beta, L1_conv_bn_mean, L1_conv_bn_var)]).T,
    }
    arrays = {name: np.ascontiguousarray(a) for name, a in arrays.items()}
    nc = bacc.Bacc("TRN2", target_bir_lowering=False, num_devices=1)
    aps = {name: nc.dram_tensor(f"in_{name}", a.shape, mybir.dt.from_np(a.dtype), kind="ExternalInput").ap()
           for name, a in arrays.items()}
    out = nc.dram_tensor("out", (BATCH, CHANNELS, PIXELS), F32, kind="ExternalOutput").ap()
    conv_attention(nc, out=out, **aps)
    r = run_bass_kernel_spmd(nc, [{f"in_{name}": a for name, a in arrays.items()}], core_ids=[0])
    return r.results[0]["out"].reshape(x.shape)
```

```python
import concourse.bass as bass
from concourse import mybir
from contextlib import ExitStack

F32 = mybir.dt.float32
F32R = mybir.dt.float32r
ALU = mybir.AluOpType
ACT = mybir.ActivationFunctionType
AX = mybir.AxisListType

P = 128
BATCH, CHANNELS, SIDE = 16, 512, 32
PIXELS = SIDE * SIDE
PITCH = SIDE + 2
PADDED = PITCH * PITCH
BLOCKS = CHANNELS // P
HALF = PIXELS // 2
HALF_ROWS = SIDE // 2
HIDDEN, MODEL_CH, WINDOW = 64, 16, 144
MODELS = 32
GROUPS = BLOCKS
PAIRS = 4
SLOTS = 2 * GROUPS
GROUP_CHUNKS = 9
SHIFTS = [(0, 0)] + [(r, c) for r in (-1, 0, 1) for c in (-1, 0, 1) if (r, c) != (0, 0)]
QBLOCKS = PIXELS // P
QUARTER = 2 * P
QUARTERS = PIXELS // QUARTER
ROWS_HELD = 4
ARRIVAL = (1, 3, 0, 2)
BY_VECTOR = 2
BAND = 32
STACK_ROWS = 3 * BAND
BN_EPS = 1e-5


def pair_order(s):
    return (0, 1, 2, 3) if s == 0 else (0, 3, 1, 2)


def conv_attention(nc, x, w1_rows, w2_t, proj_t, ww, per_channel, out):
    with ExitStack() as ctx:
        def sb(name, shape, dt=F32):
            return ctx.enter_context(nc.sbuf_tensor(name, shape, dt))

        def sem(name):
            return ctx.enter_context(nc.semaphore(name))

        xp = sb("xp", [P, BLOCKS, PADDED])
        xp_hi = sb("xp_hi", [P, BLOCKS, PADDED], F32R)
        xp_lo = sb("xp_lo", [P, BLOCKS, PADDED], F32R)
        x1 = sb("x1", [P, BLOCKS, PIXELS])
        x1_hi = sb("x1_hi", [P, BLOCKS, PIXELS], F32R)
        x1_lo = sb("x1_lo", [P, BLOCKS, PIXELS], F32R)
        hidden = sb("hidden", [P, PAIRS, HALF])
        w_first = sb("w_first", [P, GROUPS, PAIRS, HIDDEN])
        w_last = sb("w_last", [P, GROUPS, PAIRS, HIDDEN])
        w_mid_hi = sb("w_mid_hi", [P, GROUPS, PAIRS, P], F32R)
        w_mid_lo = sb("w_mid_lo", [P, GROUPS, PAIRS, P], F32R)
        w2s = sb("w2s", [P, GROUPS * PAIRS, 2 * MODEL_CH])
        wp_hi = sb("wp_hi", [P, 3, BLOCKS, P], F32R)
        wp_lo = sb("wp_lo", [P, 3, BLOCKS, P], F32R)
        ww_hi = sb("ww_hi", [P, CHANNELS], F32R)
        ww_lo = sb("ww_lo", [P, CHANNELS], F32R)
        w_stack = sb("w_stack", [STACK_ROWS, GROUPS, 3, HIDDEN], F32R)
        arena = sb("arena", [P, 10 * PIXELS], F32R)
        probs = sb("probs", [P, 2, PIXELS])
        y_hi = sb("y_hi", [P, QUARTER], F32R)
        y_lo = sb("y_lo", [P, QUARTER], F32R)
        ident = sb("ident", [P, P])
        columns = sb("columns", [P, per_channel.shape[1]])
        b1s, b2s, pbs = columns[:, 0:16], columns[:, 16:20], columns[:, 20:23]
        bn = columns[:, 23:43].rearrange("p (v k) -> p v k", v=5)
        inv = sb("inv", [P, BLOCKS])
        shift = sb("shift", [P, BLOCKS])
        bn_a = sb("bn_a", [P, BLOCKS])
        bn_b = sb("bn_b", [P, BLOCKS])
        neg_max = sb("neg_max", [P, 2])
        row_sum = sb("row_sum", [P, ROWS_HELD])
        row_inv = sb("row_inv", [P, ROWS_HELD])
        held = sb("held", [P, GROUPS + 2])

        def in_arena(at, blocks, cols):
            return arena[:, at * PIXELS:at * PIXELS + blocks * cols].rearrange("p (b c) -> p b c", b=blocks)

        tp_hi, tp_lo = in_arena(0, 2, PIXELS), in_arena(2, 2, PIXELS)
        pt_hi, pt_lo = in_arena(4, QBLOCKS, QUARTER), in_arena(6, QBLOCKS, QUARTER)
        g_hi, g_lo = in_arena(8, QBLOCKS, P), in_arena(9, QBLOCKS, P)

        LOW, HIGH = 0, 1

        def stack_of(grp, band):
            at = (2 * ((grp - 1) % GROUPS) + band) * PADDED
            return arena[0:STACK_ROWS, at:at + PADDED]

        def stack_block(grp):
            return (GROUP_CHUNKS * grp + 2) % BLOCKS

        assert 2 * PADDED <= 4 * PIXELS
        assert 2 * GROUPS * PADDED <= 10 * PIXELS

        hidden_halves = hidden[:, :, :].rearrange("p q n -> p (q n)").rearrange("p (s n) -> p s n", s=2)
        softmax_rows = [probs[:, 0, :], probs[:, 1, :], hidden_halves[:, 0, :], hidden_halves[:, 1, :]]
        g_t = hidden_halves[:, 1, :]

        def stage(n, a):
            whole = isinstance(n, int) and n == 0
            return softmax_rows[a if whole else min(a, 2)]

        mid_raw = x1[:, 0:2, :].rearrange("p k n -> p (k n)").rearrange("p (g q m) -> p g q m", g=GROUPS, q=PAIRS)
        w_stack_raw = x1[0:STACK_ROWS, 0, 0:3 * GROUPS * HIDDEN].rearrange(
            "p (g v d) -> p g v d", g=GROUPS, v=3)
        wp_raw = x1[:, 2:4, :].rearrange("p k n -> p (k n)")[:, 0:3 * BLOCKS * P].rearrange(
            "p (w k o) -> p w k o", w=3, k=BLOCKS)
        ww_raw = x1[:, 3, PIXELS - BLOCKS * P:PIXELS].rearrange("p (k o) -> p k o", k=BLOCKS)

        ps = ctx.enter_context(nc.psum_tensor("ps", [P, 8, HALF], F32))
        BANK_T, BANK_Y, BANK_DX = 4, 6, 7

        def y_bank(j):
            return BANK_Y + j % 2

        def z_bank(j, v):
            return y_bank(j + 1 - v)

        score_banks = [ps[:, 0:2, :], ps[:, 2:4, :]]

        def padded(t, k):
            return t[:, k, :].rearrange("p (h w) -> p h w", w=PITCH)

        padded_all = xp[:, :, :].rearrange("p k (h w) -> p k h w", w=PITCH)

        def shifted_in(image, chunk, half):
            dr, dc = SHIFTS[chunk // BLOCKS]
            r0 = 1 + dr + HALF_ROWS * half
            return image.rearrange("p (h w) -> p h w", w=PITCH)[:, r0:r0 + HALF_ROWS, 1 + dc:1 + dc + SIDE]

        def shifted(t, chunk, half):
            return shifted_in(t[:, chunk % BLOCKS, :], chunk, half)

        def inside(t, k):
            return padded(t, k)[:, 1:1 + SIDE, 1:1 + SIDE]

        w_mid_loaded = sem("w_mid_loaded")
        w_l0_loaded = sem("w_l0_loaded")
        w_stack_loaded = sem("w_stack_loaded")
        w_l1_loaded = sem("w_l1_loaded")
        borders_zero = sem("borders_zero")
        w_mid_zero = sem("w_mid_zero")
        weights_zero = sem("weights_zero")
        ident_zero = sem("ident_zero")
        ident_ready = sem("ident_ready")
        w_mid_rounded = sem("w_mid_rounded")
        w_mid_split = sem("w_mid_split")
        w_stack_zero = sem("w_stack_zero")
        w_stack_rounded = sem("w_stack_rounded")
        w_stack_split = sem("w_stack_split")
        wp_rounded = sem("wp_rounded")
        wp_split = sem("wp_split")
        bn_step = sem("bn_step")
        var_ready = sem("var_ready")
        std_ready = sem("std_ready")
        ww_scaled = sem("ww_scaled")
        ww_transposed = sem("ww_transposed")
        ww_rounded = sem("ww_rounded")
        ww_split = sem("ww_split")

        x_loaded = [sem(f"x_loaded_{a}") for a in range(BLOCKS)]
        xp_copied = sem("xp_copied")
        xp_rounded = sem("xp_rounded")
        xp_split_odd = sem("xp_split_odd")
        xp_split_even = sem("xp_split_even")
        stacked = [sem(f"stacked_{g}") for g in range(GROUPS)]
        hidden_summed = sem("hidden_summed")
        hidden_ready = sem("hidden_ready")
        dx_summed = sem("dx_summed")
        x1_ready = sem("x1_ready")
        x1_rounded = sem("x1_rounded")
        x1_split = sem("x1_split")
        projected = sem("projected")
        proj_biased = sem("proj_biased")
        tp_split = sem("tp_split")
        scored = sem("scored")
        max_found = sem("max_found")
        exp_done = sem("exp_done")
        inv_done = sem("inv_done")
        normalized = sem("normalized")
        transposed = sem("transposed")
        t_rounded = sem("t_rounded")
        t_split = sem("t_split")
        y_summed = sem("y_summed")
        y_rounded = sem("y_rounded")
        y_split = sem("y_split")
        z_summed = sem("z_summed")
        out_added = sem("out_added")
        stored = [sem("stored_0"), sem("stored_1")]

        TH, PH, G = 0, 1, 2
        PROJECTIONS = [(0, TH, 4), (0, PH, 5), (1, PH, 4), (0, G, 5), (1, G, 4), (1, TH, 6)]
        TP_ORDER = [p[:2] for p in PROJECTIONS if p[1] != G]

        def proj_step(half, w):
            return [p[:2] for p in PROJECTIONS].index((half, w))

        T_PER = 2 * (QBLOCKS + 1)

        block = ctx.enter_context(nc.Block())

        @block.sync
        def _(sp):
            def load_x(n, a):
                k = ARRIVAL[a]
                sp.dma_start(stage(n, a), x[n, k * P:(k + 1) * P, :]).then_inc(x_loaded[a], 16)

            def load_first_blocks(n):
                sp.wait_ge(transposed, (n - 1) * T_PER)
                load_x(n, 0)
                load_x(n, 1)

            def store_quarter(n, j):
                sp.wait_ge(out_added, n * 8 + 2 * j + 2)
                sp.dma_start(out[n, :, j * QUARTER:(j + 1) * QUARTER].rearrange("(k p) n -> p k n", p=P),
                             x1[:, :, j * QUARTER:(j + 1) * QUARTER]).then_inc(stored[j // 2], 16)

            def batch(n, has_next, has_second):
                if has_next:
                    sp.wait_ge(dx_summed, n * SLOTS + SLOTS)
                    load_x(n + 1, 2)
                    sp.wait_ge(xp_copied, (n + 1) * BLOCKS + 3)
                    load_x(n + 1, 3)
                for j in range(QUARTERS):
                    store_quarter(n, j)
                if has_second:
                    load_first_blocks(n + 2)

            load_x(0, 0)
            load_x(0, 1)
            rows = w1_rows.rearrange("(g r) d -> r g d", g=GROUPS)
            sp.wait_ge(w_mid_zero, 1)
            for q in range(PAIRS):
                at, cut = 2 * P * q, 32 * q + 16
                sp.dma_start(mid_raw[0:cut, :, q, 0:HIDDEN], rows[at + P:at + P + cut]).then_inc(w_mid_loaded, 16)
                sp.dma_start(mid_raw[cut:P, :, q, HIDDEN:P], rows[at + P + cut:at + 2 * P]).then_inc(w_mid_loaded, 16)
            load_x(0, 2)
            load_x(0, 3)
            sp.wait_ge(weights_zero, 1)
            for q in range(PAIRS):
                at = 2 * P * q
                sp.dma_start(w_first[32 * q:P, :, q, :], rows[at + 32 * q:at + P]).then_inc(w_l0_loaded, 16)
                sp.dma_start(w_last[0:32 * q + 32, :, q, :],
                             rows[at + 2 * P:at + 2 * P + 32 * q + 32]).then_inc(w_l0_loaded, 16)
            for half in range(2):
                sp.dma_start(w2s[half * HIDDEN:(half + 1) * HIDDEN, :, half * MODEL_CH:(half + 1) * MODEL_CH],
                             w2_t[half].rearrange("m d c -> d m c")).then_inc(w_l0_loaded, 16)
            sp.dma_start(columns[:, :], per_channel).then_inc(w_l0_loaded, 16)
            for w in range(3):
                sp.dma_start(wp_raw[:, w, :, :], proj_t[w].rearrange("(k p) o -> p k o", p=P)).then_inc(w_l1_loaded, 16)
            sp.dma_start(ww_raw, ww.rearrange("(k p) o -> p k o", p=P)).then_inc(w_l1_loaded, 16)
            sp.wait_ge(w_stack_zero, 1)
            for part in range(3):
                place = w_stack_raw[part * BAND:(part + 1) * BAND]
                sp.dma_start(place[:, :, 2, :], rows[2 * P:2 * P + BAND]).then_inc(w_stack_loaded, 16)
                sp.dma_start(place[:, :, 0, :], rows[7 * P - BAND:7 * P]).then_inc(w_stack_loaded, 16)

            sp.wait_ge(xp_copied, 2)
            load_x(1, 0)
            load_x(1, 1)

            with sp.Fori(0, BATCH - 2) as n:
                batch(n, True, True)
            batch(BATCH - 2, True, False)
            batch(BATCH - 1, False, False)
            for s in stored:
                sp.wait_ge(s, 16 * 2 * BATCH)

        W_MID_DMAS, W_L0_DMAS, W_L1_DMAS = 2 * PAIRS, 2 * PAIRS + 3, 4

        @block.tensor
        def _(pe):
            mm = nc.tensor.matmul

            def hidden_mid(n, s, q):
                half, grp = divmod(s, GROUPS)
                chunk = GROUP_CHUNKS * grp + 2 * q + 1
                if s > 0:
                    pe.wait_ge(hidden_ready, (n * SLOTS + s - 1) * PAIRS + pair_order(s - 1).index(q) + 1)
                elif q < 2:
                    pe.wait_ge(xp_split_odd, n * BY_VECTOR + q + 1)
                if s == 1 and q == pair_order(0)[0]:
                    pe.wait_ge(xp_split_even, (n + 1) * (BLOCKS - BY_VECTOR))
                mid_hi, mid_lo = w_mid_hi[:, grp, q, :], w_mid_lo[:, grp, q, :]
                for i, (w, image) in enumerate(((mid_hi, xp_hi), (mid_hi, xp_lo), (mid_lo, xp_hi))):
                    mm(ps[:, q, :], w, shifted(image, chunk, half), start=(i == 0), stop=False, skip_group_check=True)

            def hidden_ends(n, s, q):
                half, grp = divmod(s, GROUPS)
                chunk = GROUP_CHUNKS * grp + 2 * q
                if s == 0 and q == 0:
                    pe.wait_ge(xp_copied, (n + 1) * BLOCKS)
                mm(ps[0:HIDDEN, q, :], w_first[:, grp, q, :], shifted(xp, chunk, half), start=False, stop=True,
                   skip_group_check=True)
                mm(ps[HIDDEN:P, q, :], w_last[:, grp, q, :], shifted(xp, chunk + 2, half), start=False, stop=True,
                   skip_group_check=True).then_inc(hidden_summed, 1)

            def hidden_stacked(n, s):
                half, grp = divmod(s, GROUPS)
                if s <= GROUPS:
                    pe.wait_ge(stacked[grp], (n + 1) * 6 * 16)
                w = w_stack[:, grp, :, :].rearrange("p v d -> p (v d)")
                for q, band, chunk, w_cols in ((0, LOW, 2, w[:, HIDDEN:3 * HIDDEN]), (3, HIGH, 6, w[:, 0:2 * HIDDEN])):
                    mm(ps[:, q, :], w_cols, shifted_in(stack_of(grp, band), GROUP_CHUNKS * grp + chunk, half),
                       start=False, stop=False, skip_group_check=True)

            def hidden_outer(n, s):
                half, grp = divmod(s, GROUPS)
                chunk = GROUP_CHUNKS * grp
                mm(ps[0:HIDDEN, 0, :], w_first[:, grp, 0, :], shifted(xp, chunk, half), start=False, stop=True,
                   skip_group_check=True).then_inc(hidden_summed, 1)
                mm(ps[HIDDEN:P, 3, :], w_last[:, grp, 3, :], shifted(xp, chunk + GROUP_CHUNKS - 1, half),
                   start=False, stop=True, skip_group_check=True).then_inc(hidden_summed, 1)

            def dx(n, s):
                pe.wait_ge(hidden_ready, n * SLOTS * PAIRS + (s + 1) * PAIRS)
                if s > 0:
                    pe.wait_ge(x1_ready, n * SLOTS + s)
                elif not (isinstance(n, int) and n == 0):
                    pe.wait_ge(out_added, n * 8)
                for q in range(PAIRS):
                    last = mm(ps[32 * q:32 * q + 32, BANK_DX, :], w2s[:, (s % GROUPS) * PAIRS + q, :],
                              hidden[:, q, :], start=True, stop=True)
                last.then_inc(dx_summed, 1)

            def project(n, half, w):
                step = proj_step(half, w)
                bank = ps[:, PROJECTIONS[step][2], :]
                if step in (0, 2):
                    pe.wait_ge(x1_split, n * SLOTS + GROUPS * (half + 1))
                if 2 <= step < 5:
                    pe.wait_ge(tp_split, n * 4 + step - 1)
                cols = slice(half * HALF, (half + 1) * HALF)
                for k in range(BLOCKS):
                    mm(bank, wp_hi[:, w, k, :], x1_hi[:, k, cols], start=(k == 0), stop=False)
                    mm(bank, wp_hi[:, w, k, :], x1_lo[:, k, cols], start=False, stop=False)
                    last = mm(bank, wp_lo[:, w, k, :], x1_hi[:, k, cols], start=False, stop=(k == BLOCKS - 1))
                last.then_inc(projected, 1)

            def scores(n, i):
                if i == 0:
                    pe.wait_ge(tp_split, n * 4 + 3)
                if i == QBLOCKS // 2:
                    pe.wait_ge(tp_split, n * 4 + 4)
                if i >= 2:
                    pe.wait_ge(exp_done, n * QBLOCKS + i - 1)
                rows = slice(i * P, (i + 1) * P)
                for half in range(2):
                    bank, cols = ps[:, 2 * (i % 2) + half, :], slice(half * HALF, (half + 1) * HALF)
                    mm(bank, tp_hi[:, TH, rows], tp_hi[:, PH, cols], start=True, stop=False)
                    mm(bank, tp_hi[:, TH, rows], tp_lo[:, PH, cols], start=False, stop=False)
                    last = mm(bank, tp_lo[:, TH, rows], tp_hi[:, PH, cols], start=False, stop=True)
                last.then_inc(scored, 1)

            def transpose(n, tau):
                for u in range(2):
                    if tau == 0:
                        src = g_t
                        if u == 0:
                            pe.wait_ge(proj_biased, n * 6 + 5)
                    else:
                        if u == 0:
                            pe.wait_ge(normalized, n * QBLOCKS + tau)
                        pe.wait_ge(t_split, n * T_PER + 2 * (tau - 1) + u + 1)
                        src = softmax_rows[(tau - 1) % ROWS_HELD]
                    for v in range(4):
                        c = (4 * u + v) * P
                        last = nc.tensor.transpose(ps[:, BANK_T + u, v * P:(v + 1) * P], src[:, c:c + P], ident[:, :])
                    last.then_inc(transposed, 1)

            def attend(n, j):
                if j > 0:
                    pe.wait_ge(out_added, n * 8 + 2 * j - 1)
                bank = ps[:, y_bank(j), 0:QUARTER]
                for m in range(QBLOCKS):
                    if m % 4 == 0:
                        pe.wait_ge(t_split, n * T_PER + 2 * (2 * j + 2) + m // 4 + 1)
                    mm(bank, g_hi[:, m, :], pt_hi[:, m, :], start=(m == 0), stop=False)
                    mm(bank, g_hi[:, m, :], pt_lo[:, m, :], start=False, stop=False)
                    last = mm(bank, g_lo[:, m, :], pt_hi[:, m, :], start=False, stop=(m == QBLOCKS - 1))
                last.then_inc(y_summed, 1)

            def output(n, j, v):
                if v == 0:
                    pe.wait_ge(y_rounded, n * QUARTERS + j + 1)
                    if j > 0:
                        pe.wait_ge(out_added, n * 8 + 2 * j)
                places = [ps[:, z_bank(j, v), e * QUARTER:(e + 1) * QUARTER] for e in range(2)]
                for e in range(2):
                    c = slice((2 * v + e) * P, (2 * v + e + 1) * P)
                    mm(places[e], ww_hi[:, c], y_hi[:, :], start=(e == 0), stop=False, skip_group_check=True)
                    mm(places[e], ww_lo[:, c], y_hi[:, :], start=False, stop=False, skip_group_check=True)
                if v == 0:
                    pe.wait_ge(y_split, n * QUARTERS + j + 1)
                for e in range(2):
                    c = slice((2 * v + e) * P, (2 * v + e + 1) * P)
                    last = mm(places[e], ww_hi[:, c], y_lo[:, :], start=False, stop=True, skip_group_check=True)
                last.then_inc(z_summed, 1)

            def image_slot(n, s):
                for q in pair_order(s - 1):
                    hidden_mid(n, s, q)
                hidden_stacked(n, s)
                hidden_outer(n, s)
                dx(n, s - 1)
                hidden_ends(n, s, 1)
                hidden_ends(n, s, 2)

            def batch(n, has_next):
                project(n, 0, TH)
                dx(n, SLOTS - 1)
                project(n, 0, PH)
                project(n, 1, PH)
                project(n, 0, G)
                scores(n, 0)
                project(n, 1, G)
                scores(n, 1)
                transpose(n, 0)
                for i in range(QBLOCKS):
                    j = i // 2
                    if i % 2 == 0:
                        if i + 2 < QBLOCKS:
                            scores(n, i + 2)
                        elif has_next:
                            hidden_mid(n + 1, 0, 0)
                            hidden_mid(n + 1, 0, 1)
                        if j > 0:
                            attend(n, j - 1)
                        transpose(n, i + 1)
                        if i == 0:
                            project(n, 1, TH)
                    else:
                        if j > 0:
                            output(n, j - 1, 0)
                        if i + 2 < QBLOCKS:
                            scores(n, i + 2)
                        elif has_next:
                            hidden_mid(n + 1, 0, 2)
                            hidden_mid(n + 1, 0, 3)
                        transpose(n, i + 1)
                        if j > 0:
                            output(n, j - 1, 1)
                if has_next:
                    hidden_ends(n + 1, 0, 0)
                    hidden_ends(n + 1, 0, 1)
                attend(n, QUARTERS - 1)
                if has_next:
                    hidden_ends(n + 1, 0, 2)
                    hidden_ends(n + 1, 0, 3)
                output(n, QUARTERS - 1, 0)
                output(n, QUARTERS - 1, 1)
                if has_next:
                    for s in range(1, SLOTS):
                        image_slot(n + 1, s)

            pe.wait_ge(w_mid_split, 1)
            for q in range(PAIRS):
                hidden_mid(0, 0, q)
            pe.wait_ge(w_l0_loaded, 16 * W_L0_DMAS)
            for q in range(PAIRS):
                hidden_ends(0, 0, q)
            pe.wait_ge(w_stack_split, 1)
            for s in range(1, GROUPS):
                pe.wait_ge(w_mid_split, s + 1)
                image_slot(0, s)
            pe.wait_ge(ident_ready, 1)
            pe.wait_ge(ww_scaled, BLOCKS)
            for k in range(BLOCKS):
                last = nc.tensor.transpose(ps[:, BANK_Y, k * P:(k + 1) * P], ww_raw[:, k, :], ident[:, :])
            last.then_inc(ww_transposed, 1)
            for s in range(GROUPS, SLOTS):
                image_slot(0, s)
            pe.wait_ge(wp_split, 1)
            pe.wait_ge(ww_split, 1)
            with pe.Fori(0, BATCH - 1) as n:
                batch(n, True)
            batch(BATCH - 1, False)

        @block.scalar
        def _(act):
            activation = nc.scalar.activation

            def relu(n, s, q):
                act.wait_ge(hidden_summed, (n * SLOTS + s) * PAIRS + pair_order(s).index(q) + 1)
                if q == 0 and s > 0:
                    act.wait_ge(dx_summed, n * SLOTS + s)
                grp = s % GROUPS
                activation(hidden[:, q, :], ps[:, q, :], ACT.Relu,
                           bias=b1s[:, grp * PAIRS + q:grp * PAIRS + q + 1]).then_inc(hidden_ready, 1)

            def round_x1(n, s):
                half, grp = divmod(s, GROUPS)
                act.wait_ge(x1_ready, n * SLOTS + s + 1)
                cols = slice(half * HALF, (half + 1) * HALF)
                nc.scalar.copy(x1_hi[:, grp, cols], x1[:, grp, cols]).then_inc(x1_rounded, 1)

            def bias_projection(n, half, w):
                step = proj_step(half, w)
                act.wait_ge(projected, n * 6 + step + 1)
                cols = slice(half * HALF, (half + 1) * HALF)
                if w == G:
                    act.wait_ge(dx_summed, n * SLOTS + SLOTS)
                dst = g_t[:, cols] if w == G else tp_hi[:, w, cols]
                activation(dst, ps[:, PROJECTIONS[step][2], :], ACT.Identity,
                           bias=pbs[:, w:w + 1]).then_inc(proj_biased, 1)

            def exp_rows(n, i):
                act.wait_ge(max_found, n * QBLOCKS + i + 1)
                if i < 3:
                    act.wait_ge(xp_copied, last_x_copied(n, i))
                else:
                    act.wait_ge(transposed, n * T_PER + 2 * (i - ROWS_HELD) + 4)
                e = slice(i % ROWS_HELD, i % ROWS_HELD + 1)
                activation(softmax_rows[i % ROWS_HELD], score_banks[i % 2], ACT.Exp,
                           bias=neg_max[:, i % 2:i % 2 + 1], accum_out=row_sum[:, e]).then_inc(exp_done, 1)

            def last_x_copied(n, i):
                if isinstance(n, int) and n == BATCH - 1:
                    return BATCH * BLOCKS
                return (n + 1) * BLOCKS + (i + 1 if i < 2 else BLOCKS)

            def round_transposed(n, tau):
                for u in range(2):
                    act.wait_ge(transposed, n * T_PER + 2 * tau + u + 1)
                    src = ps[:, BANK_T + u, :].rearrange("p (m n) -> p m n", m=4)
                    if tau == 0:
                        dst = g_hi[:, 4 * u:4 * u + 4, :]
                    else:
                        if u == 0 and tau >= 3 and tau % 2 == 1:
                            act.wait_ge(y_summed, n * QUARTERS + (tau - 1) // 2)
                        c = (tau - 1) % 2 * P
                        dst = pt_hi[:, 4 * u:4 * u + 4, c:c + P]
                    nc.scalar.copy(dst, src).then_inc(t_rounded, 1)

            def round_y(n, j):
                act.wait_ge(y_summed, n * QUARTERS + j + 1)
                if j > 0:
                    act.wait_ge(z_summed, n * 8 + 2 * j)
                nc.scalar.copy(y_hi[:, :], ps[:, y_bank(j), 0:QUARTER]).then_inc(y_rounded, 1)

            def round_image(n, a):
                act.wait_ge(xp_copied, n * BLOCKS + a + 1)
                nc.scalar.copy(xp_hi[:, ARRIVAL[a], :], xp[:, ARRIVAL[a], :]).then_inc(xp_rounded, 1)

            def image_slot(n, s):
                order = pair_order(s)
                relu(n, s, order[0])
                relu(n, s, order[1])
                round_x1(n, s - 1)
                relu(n, s, order[2])
                relu(n, s, order[3])

            def batch(n, has_next):
                bias_projection(n, 0, TH)
                round_x1(n, SLOTS - 1)
                bias_projection(n, 0, PH)
                if has_next:
                    round_image(n + 1, 0)
                bias_projection(n, 1, PH)
                if has_next:
                    round_image(n + 1, 1)
                bias_projection(n, 0, G)
                if has_next:
                    round_image(n + 1, 2)
                bias_projection(n, 1, G)
                exp_rows(n, 0)
                round_transposed(n, 0)
                exp_rows(n, 1)
                exp_rows(n, 2)
                for i in range(QBLOCKS):
                    j = i // 2
                    if i % 2 == 0 and j > 0:
                        if i + 2 < QBLOCKS:
                            exp_rows(n, i + 2)
                        round_y(n, j - 1)
                        round_transposed(n, i + 1)
                    else:
                        round_transposed(n, i + 1)
                        if i == 0:
                            bias_projection(n, 1, TH)
                        if 2 < i + 2 < QBLOCKS:
                            exp_rows(n, i + 2)
                    if i == 6 and has_next:
                        round_image(n + 1, 3)
                if has_next:
                    relu(n + 1, 0, 0)
                    relu(n + 1, 0, 1)
                round_y(n, QUARTERS - 1)
                if has_next:
                    relu(n + 1, 0, 2)
                    relu(n + 1, 0, 3)
                    for s in range(1, SLOTS):
                        image_slot(n + 1, s)

            round_image(0, 0)
            act.wait_ge(w_mid_loaded, 16 * W_MID_DMAS)
            for grp in range(GROUPS):
                nc.scalar.copy(w_mid_hi[:, grp, :, :], mid_raw[:, grp, :, :]).then_inc(w_mid_rounded, 1)
                if grp < BLOCKS - 1:
                    round_image(0, grp + 1)
            act.wait_ge(w_l0_loaded, 16 * W_L0_DMAS)
            for q in range(PAIRS):
                relu(0, 0, q)
            act.wait_ge(w_stack_loaded, 6 * 16)
            nc.scalar.copy(w_stack[:, :, :, :], w_stack_raw).then_inc(w_stack_rounded, 1)
            act.wait_ge(w_l1_loaded, 16 * W_L1_DMAS)
            nc.scalar.copy(wp_hi[:, :, :, :], wp_raw).then_inc(wp_rounded, 1)
            act.wait_ge(var_ready, 1)
            nc.scalar.sqrt(bn_b[:, :], bn_a[:, :]).then_inc(std_ready, 1)
            nc.scalar.preload_act_table(ACT.Exp)
            for s in range(1, GROUPS):
                image_slot(0, s)
            act.wait_ge(ww_transposed, 1)
            nc.scalar.copy(ww_hi[:, :], ps[:, BANK_Y, :]).then_inc(ww_rounded, 1)
            for s in range(GROUPS, SLOTS):
                image_slot(0, s)
            with act.Fori(0, BATCH - 1) as n:
                batch(n, True)
            batch(BATCH - 1, False)

        @block.vector
        def _(dve):
            stt = nc.vector.scalar_tensor_tensor

            def sum_x1(n, s):
                half, grp = divmod(s, GROUPS)
                dve.wait_ge(dx_summed, n * SLOTS + s + 1)
                image = inside(xp, grp)[:, half * HALF_ROWS:(half + 1) * HALF_ROWS, :]
                stt(out=x1[:, grp, half * HALF:(half + 1) * HALF].rearrange("p (h w) -> p h w", w=SIDE),
                    in0=ps[:, BANK_DX, :].rearrange("p (h w) -> p h w", w=SIDE), scalar=b2s[:, grp:grp + 1],
                    in1=image, op0=ALU.add, op1=ALU.add).then_inc(x1_ready, 1)

            def split_x1(n, s):
                half, grp = divmod(s, GROUPS)
                cols = slice(half * HALF, (half + 1) * HALF)
                dve.wait_ge(x1_rounded, n * SLOTS + s + 1)
                nc.vector.tensor_tensor(x1_lo[:, grp, cols], x1[:, grp, cols], x1_hi[:, grp, cols].bitcast(F32),
                                        ALU.subtract).then_inc(x1_split, 1)

            def split_projection(n, half, w):
                step = proj_step(half, w)
                dve.wait_ge(proj_biased, n * 6 + step + 1)
                cols = slice(half * HALF, (half + 1) * HALF)
                stt(out=tp_lo[:, w, cols], in0=ps[:, PROJECTIONS[step][2], :], scalar=pbs[:, w:w + 1],
                    in1=tp_hi[:, w, cols].bitcast(F32), op0=ALU.add, op1=ALU.subtract).then_inc(tp_split, 1)

            def copy_image(n, a):
                dve.wait_ge(x_loaded[a], (n + 1) * 16)
                nc.vector.tensor_copy(inside(xp, ARRIVAL[a]), stage(n, a).rearrange("p (h w) -> p h w", w=SIDE)
                                      ).then_inc(xp_copied, 1)

            def split_image(n, a):
                k = ARRIVAL[a]
                dve.wait_ge(xp_rounded, n * BLOCKS + a + 1)
                nc.vector.tensor_tensor(xp_lo[:, k, :], xp[:, k, :], xp_hi[:, k, :].bitcast(F32),
                                        ALU.subtract).then_inc(xp_split_odd, 1)

            def find_max(n, i):
                dve.wait_ge(scored, n * QBLOCKS + i + 1)
                nc.vector.tensor_reduce(neg_max[:, i % 2:i % 2 + 1], score_banks[i % 2], op=ALU.max, axis=AX.XY,
                                        negate=True).then_inc(max_found, 1)

            def invert_sum(n, i):
                e = slice(i % ROWS_HELD, i % ROWS_HELD + 1)
                dve.wait_ge(exp_done, n * QBLOCKS + i + 1)
                nc.vector.reciprocal(row_inv[:, e], row_sum[:, e]).then_inc(inv_done, 1)

            def split_transposed(n, tau):
                for u in range(2):
                    dve.wait_ge(t_rounded, n * T_PER + 2 * tau + u + 1)
                    src = ps[:, BANK_T + u, :].rearrange("p (m n) -> p m n", m=4)
                    if tau == 0:
                        hi, lo = (t[:, 4 * u:4 * u + 4, :] for t in (g_hi, g_lo))
                    else:
                        c = (tau - 1) % 2 * P
                        hi, lo = (t[:, 4 * u:4 * u + 4, c:c + P] for t in (pt_hi, pt_lo))
                    nc.vector.tensor_tensor(lo, src, hi.bitcast(F32), ALU.subtract).then_inc(t_split, 1)

            def split_y(n, j):
                dve.wait_ge(y_rounded, n * QUARTERS + j + 1)
                nc.vector.tensor_tensor(y_lo[:, :], ps[:, y_bank(j), 0:QUARTER], y_hi[:, :].bitcast(F32),
                                        ALU.subtract).then_inc(y_split, 1)

            def add_out(n, j, v):
                dve.wait_ge(z_summed, n * 8 + 2 * j + v + 1)
                for e in range(2):
                    k = 2 * v + e
                    place = x1[:, k, j * QUARTER:(j + 1) * QUARTER]
                    last = stt(out=place, in0=ps[:, z_bank(j, v), e * QUARTER:(e + 1) * QUARTER],
                               scalar=shift[:, k:k + 1], in1=place, op0=ALU.add, op1=ALU.add)
                last.then_inc(out_added, 1)

            def batch(n, has_next):
                split_projection(n, 0, TH)
                sum_x1(n, SLOTS - 1)
                split_x1(n, SLOTS - 1)
                if has_next:
                    dve.wait_ge(hidden_summed, (n + 1) * SLOTS * PAIRS)
                    copy_image(n + 1, 0)
                split_projection(n, 0, PH)
                if has_next:
                    copy_image(n + 1, 1)
                    split_image(n + 1, 0)
                    copy_image(n + 1, 2)
                split_projection(n, 1, PH)
                if has_next:
                    split_image(n + 1, 1)
                    copy_image(n + 1, 3)
                find_max(n, 0)
                invert_sum(n, 0)
                find_max(n, 1)
                split_transposed(n, 0)
                find_max(n, 2)
                invert_sum(n, 1)
                split_transposed(n, 1)
                split_projection(n, 1, TH)
                for i in range(1, QBLOCKS):
                    j = i // 2
                    if i + 1 < QBLOCKS:
                        invert_sum(n, i + 1)
                    if i % 2 == 1 and j > 0:
                        add_out(n, j - 1, 0)
                    if i + 2 < QBLOCKS:
                        find_max(n, i + 2)
                    if i % 2 == 0 and j > 0:
                        split_y(n, j - 1)
                    split_transposed(n, i + 1)
                    if i % 2 == 1 and j > 0:
                        add_out(n, j - 1, 1)
                split_y(n, QUARTERS - 1)
                add_out(n, QUARTERS - 1, 0)
                add_out(n, QUARTERS - 1, 1)
                if has_next:
                    dve.wait_ge(stored[0], (n + 1) * 32)
                    for s in range(GROUPS):
                        sum_x1(n + 1, s)
                        split_x1(n + 1, s)
                    dve.wait_ge(stored[1], (n + 1) * 32)
                    for s in range(GROUPS, SLOTS - 1):
                        sum_x1(n + 1, s)
                        split_x1(n + 1, s)

            nc.vector.memset(mid_raw, 0.0).then_inc(w_mid_zero, 1)
            dve.wait_ge(borders_zero, 1)
            copy_image(0, 0)
            copy_image(0, 1)
            split_image(0, 0)

            def split_w_mid(grp):
                dve.wait_ge(w_mid_rounded, grp + 1)
                nc.vector.tensor_tensor(w_mid_lo[:, grp, :, :], mid_raw[:, grp, :, :],
                                        w_mid_hi[:, grp, :, :].bitcast(F32), ALU.subtract).then_inc(w_mid_split, 1)

            split_w_mid(0)
            split_image(0, 1)
            copy_image(0, 2)
            copy_image(0, 3)
            split_w_mid(1)
            dve.wait_ge(w_mid_split, 2)
            nc.vector.memset(w_stack_raw, 0.0).then_inc(w_stack_zero, 1)
            for grp in range(2, GROUPS):
                split_w_mid(grp)
            dve.wait_ge(w_stack_rounded, 1)
            middle = slice(BAND, 2 * BAND)
            nc.vector.tensor_tensor(w_stack[middle], w_stack_raw[middle], w_stack[middle].bitcast(F32),
                                    ALU.subtract).then_inc(w_stack_split, 1)
            dve.wait_ge(wp_rounded, 1)
            nc.vector.tensor_tensor(wp_lo[:, :, :, :], wp_raw, wp_hi[:, :, :, :].bitcast(F32),
                                    ALU.subtract).then_inc(wp_split, 1)

            steps = [0]

            def chain(instruction):
                steps[0] += 1
                instruction.then_inc(bn_step, 1)
                dve.wait_ge(bn_step, steps[0])

            WB, GAMMA, BETA, MEAN, VAR = range(5)
            tt, ts = nc.vector.tensor_tensor, nc.vector.tensor_scalar
            dve.wait_ge(w_l0_loaded, 16 * W_L0_DMAS)
            dve.wait_ge(w_l1_loaded, 16 * W_L1_DMAS)
            ts(bn_a[:, :], bn[:, VAR, :], BN_EPS, None, ALU.add).then_inc(var_ready, 1)
            dve.wait_ge(std_ready, 1)
            chain(nc.vector.reciprocal(inv[:, :], bn_b[:, :]))
            chain(tt(bn_b[:, :], inv[:, :], inv[:, :], ALU.mult))
            chain(tt(bn_b[:, :], bn_b[:, :], bn_a[:, :], ALU.mult))
            chain(ts(bn_b[:, :], bn_b[:, :], -0.5, 1.5, ALU.mult, ALU.add))
            chain(tt(inv[:, :], inv[:, :], bn_b[:, :], ALU.mult))
            chain(tt(inv[:, :], inv[:, :], bn[:, GAMMA, :], ALU.mult))
            chain(tt(shift[:, :], bn[:, WB, :], bn[:, MEAN, :], ALU.subtract))
            chain(tt(shift[:, :], shift[:, :], inv[:, :], ALU.mult))
            chain(tt(shift[:, :], shift[:, :], bn[:, BETA, :], ALU.add))
            for k in range(BLOCKS):
                ts(ww_raw[:, k, :], ww_raw[:, k, :], inv[:, k:k + 1], None, ALU.mult).then_inc(ww_scaled, 1)
            for s in range(GROUPS - 1):
                sum_x1(0, s)
                split_x1(0, s)
            dve.wait_ge(ww_rounded, 1)
            tt(ww_lo[:, :], ps[:, BANK_Y, :], ww_hi[:, :].bitcast(F32), ALU.subtract).then_inc(ww_split, 1)
            for s in range(GROUPS - 1, SLOTS - 1):
                sum_x1(0, s)
                split_x1(0, s)
            with dve.Fori(0, BATCH - 1) as n:
                batch(n, True)
            batch(BATCH - 1, False)

        @block.gpsimd
        def _(pool):
            def normalize(n, i):
                pool.wait_ge(inv_done, n * QBLOCKS + i + 1)
                rows, e = softmax_rows[i % ROWS_HELD], slice(i % ROWS_HELD, i % ROWS_HELD + 1)
                nc.gpsimd.tensor_tensor(rows, rows, row_inv[:, e].to_broadcast([P, PIXELS]),
                                        ALU.mult).then_inc(normalized, 1)

            def split_image(n, a):
                k = ARRIVAL[a]
                pool.wait_ge(xp_rounded, n * BLOCKS + a + 1)
                nc.gpsimd.tensor_tensor(xp_lo[:, k, :], xp[:, k, :], xp_hi[:, k, :].bitcast(F32),
                                        ALU.subtract).then_inc(xp_split_even, 1)

            def hold(c):
                nc.gpsimd.tensor_tensor(held[:, c:c + 1], ident[:, 0:1], ident[:, 0:1], ALU.mult)

            def stack(n, grp):
                k = stack_block(grp)
                a = ARRIVAL.index(k)
                if a < BY_VECTOR:
                    pool.wait_ge(xp_split_odd, n * BY_VECTOR + a + 1)
                else:
                    pool.wait_ge(xp_split_even, n * (BLOCKS - BY_VECTOR) + a - BY_VECTOR + 1)
                hold(grp)
                for band, rows in enumerate((slice(0, BAND), slice(P - BAND, P))):
                    for part, image in enumerate((xp_hi, xp_hi, xp_lo)):
                        pool.dma_start(stack_of(grp, band)[part * BAND:(part + 1) * BAND, :],
                                       image[rows, k, :]).then_inc(stacked[grp], 16)

            def batch(n, has_next):
                if has_next:
                    split_image(n + 1, 2)
                normalize(n, 0)
                for i in range(1, QBLOCKS):
                    normalize(n, i)
                if has_next:
                    pool.wait_ge(scored, (n + 1) * QBLOCKS)
                    hold(GROUPS)
                    stack(n + 1, 1)
                    split_image(n + 1, 3)
                    pool.wait_ge(y_summed, (n + 1) * QUARTERS)
                    hold(GROUPS + 1)
                    for grp in (2, 3, 0):
                        stack(n + 1, grp)

            for edge in (padded_all[:, :, 0:PITCH:PITCH - 1, :], padded_all[:, :, 1:1 + SIDE, 0:PITCH:PITCH - 1]):
                last = nc.gpsimd.memset(edge, 0.0)
            last.then_inc(borders_zero, 1)
            nc.gpsimd.memset(w_first[:, :, :, :], 0.0)
            nc.gpsimd.memset(w_last[:, :, :, :], 0.0)
            nc.gpsimd.memset(w2s[:, :, :], 0.0).then_inc(weights_zero, 1)
            nc.gpsimd.memset(ident[:, :], 0.0).then_inc(ident_zero, 1)
            pool.wait_ge(ident_zero, 1)
            nc.gpsimd.affine_select(out=ident[:, :], in_=ident[:, :], compare_op=ALU.not_equal, fill=1.0, base=0,
                                    pattern=[[-1, P]], channel_multiplier=1).then_inc(ident_ready, 1)
            split_image(0, 2)
            split_image(0, 3)
            pool.wait_ge(ident_ready, 1)
            for grp in (1, 2, 3, 0):
                stack(0, grp)
            with pool.Fori(0, BATCH - 1) as n:
                batch(n, True)
            batch(BATCH - 1, False)


def kernel(x, L0_conv_w1, L0_conv_b1, L0_conv_w2, L0_conv_b2, L1_conv_theta_w, L1_conv_theta_b, L1_conv_phi_w,
           L1_conv_phi_b, L1_conv_g_w, L1_conv_g_b, L1_conv_w_w, L1_conv_w_b, L1_conv_bn_gamma, L1_conv_bn_beta,
           L1_conv_bn_mean, L1_conv_bn_var):
    import numpy as np
    import concourse.bacc as bacc
    from concourse.bass_utils import run_bass_kernel_spmd

    x = np.asarray(x)
    arrays = {
        "x": x.reshape(BATCH, CHANNELS, PIXELS),
        "w1_rows": np.asarray(L0_conv_w1).transpose(0, 2, 1).reshape(MODELS * WINDOW, HIDDEN),
        "w2_t": np.asarray(L0_conv_w2).transpose(0, 2, 1).reshape(MODELS // 2, 2, HIDDEN, MODEL_CH).transpose(1, 0, 2, 3),
        "proj_t": np.stack([np.asarray(w).T for w in (L1_conv_theta_w, L1_conv_phi_w, L1_conv_g_w)]),
        "ww": np.asarray(L1_conv_w_w),
        "per_channel": np.concatenate([np.asarray(v).reshape(-1, P) for v in (
            L0_conv_b1, L0_conv_b2, L1_conv_theta_b, L1_conv_phi_b, L1_conv_g_b, L1_conv_w_b, L1_conv_bn_gamma,
            L1_conv_bn_beta, L1_conv_bn_mean, L1_conv_bn_var)]).T,
    }
    arrays = {name: np.ascontiguousarray(a) for name, a in arrays.items()}
    nc = bacc.Bacc("TRN2", target_bir_lowering=False, num_devices=1)
    aps = {name: nc.dram_tensor(f"in_{name}", a.shape, mybir.dt.from_np(a.dtype), kind="ExternalInput").ap()
           for name, a in arrays.items()}
    out = nc.dram_tensor("out", (BATCH, CHANNELS, PIXELS), F32, kind="ExternalOutput").ap()
    conv_attention(nc, out=out, **aps)
    r = run_bass_kernel_spmd(nc, [{f"in_{name}": a for name, a in arrays.items()}], core_ids=[0])
    return r.results[0]["out"].reshape(x.shape)
```

```python
import concourse.bass as bass
from concourse import mybir
from contextlib import ExitStack

F32 = mybir.dt.float32
F32R = mybir.dt.float32r
ALU = mybir.AluOpType
ACT = mybir.ActivationFunctionType
AX = mybir.AxisListType

P = 128
BATCH, CHANNELS, SIDE = 16, 512, 32
PIXELS = SIDE * SIDE
PITCH = SIDE + 2
PADDED = PITCH * PITCH
BLOCKS = CHANNELS // P
HALF = PIXELS // 2
HALF_ROWS = SIDE // 2
HIDDEN, MODEL_CH, WINDOW = 64, 16, 144
MODELS = 32
GROUPS = BLOCKS
PAIRS = 4
SLOTS = 2 * GROUPS
GROUP_CHUNKS = 9
SHIFTS = [(0, 0)] + [(r, c) for r in (-1, 0, 1) for c in (-1, 0, 1) if (r, c) != (0, 0)]
QBLOCKS = PIXELS // P
QUARTER = 2 * P
QUARTERS = PIXELS // QUARTER
ROWS_HELD = 4
ARRIVAL = (1, 3, 0, 2)
BY_VECTOR = 2
BAND = 32
STACK_ROWS = 3 * BAND
BN_EPS = 1e-5
FIRST, LAST = 0, 1
ENDS = [(which, grp, q) for grp in range(GROUPS) for which in (FIRST, LAST) for q in range(PAIRS)
        if grp == 0 or (which == FIRST) == (q < 2)]


def pair_order(s):
    return (0, 1, 2, 3) if s == 0 else (0, 3, 1, 2)


def conv_attention(nc, x, w_mid, w_ends, w_crosses, w_stacks, w2_pairs, proj_t, ww, per_channel, out):
    with ExitStack() as ctx:
        def sb(name, shape, dt=F32):
            return ctx.enter_context(nc.sbuf_tensor(name, shape, dt))

        def sem(name):
            return ctx.enter_context(nc.semaphore(name))

        xp = sb("xp", [P, BLOCKS, PADDED])
        xp_hi = sb("xp_hi", [P, BLOCKS, PADDED], F32R)
        xp_lo = sb("xp_lo", [P, BLOCKS, PADDED], F32R)
        x1 = sb("x1", [P, BLOCKS, PIXELS])
        x1_hi = sb("x1_hi", [P, BLOCKS, PIXELS], F32R)
        x1_lo = sb("x1_lo", [P, BLOCKS, PIXELS], F32R)
        hidden = sb("hidden", [P, PAIRS, HALF])
        w_ends_sb = sb("w_ends", [P, len(ENDS), HIDDEN])
        w_mid_hi = sb("w_mid_hi", [P, GROUPS, PAIRS, P], F32R)
        w_mid_lo = sb("w_mid_lo", [P, GROUPS, PAIRS, P], F32R)
        w_cross_hi = sb("w_cross_hi", [P, GROUPS, P], F32R)
        w_cross_lo = sb("w_cross_lo", [P, GROUPS, P], F32R)
        w2s = sb("w2s", [P, GROUPS * PAIRS, 2 * MODEL_CH])
        wp_hi = sb("wp_hi", [P, 3, BLOCKS, P], F32R)
        wp_lo = sb("wp_lo", [P, 3, BLOCKS, P], F32R)
        ww_hi = sb("ww_hi", [P, CHANNELS], F32R)
        ww_lo = sb("ww_lo", [P, CHANNELS], F32R)
        w_stack = sb("w_stack", [STACK_ROWS, GROUPS, 3, HIDDEN], F32R)
        arena = sb("arena", [P, 10 * PIXELS], F32R)
        probs = sb("probs", [P, 2, PIXELS])
        y_hi = sb("y_hi", [P, QUARTER], F32R)
        y_lo = sb("y_lo", [P, QUARTER], F32R)
        ident = sb("ident", [P, P])
        columns = sb("columns", [P, per_channel.shape[1]])
        b1s, b2s, pbs = columns[:, 0:16], columns[:, 16:20], columns[:, 20:23]
        bn = columns[:, 23:43].rearrange("p (v k) -> p v k", v=5)
        inv = sb("inv", [P, BLOCKS])
        shift = sb("shift", [P, BLOCKS])
        bn_a = sb("bn_a", [P, BLOCKS])
        bn_b = sb("bn_b", [P, BLOCKS])
        neg_max = sb("neg_max", [P, 2])
        row_sum = sb("row_sum", [P, ROWS_HELD])
        row_inv = sb("row_inv", [P, ROWS_HELD])
        held = sb("held", [P, GROUPS + 2])

        def in_arena(at, blocks, cols):
            return arena[:, at * PIXELS:at * PIXELS + blocks * cols].rearrange("p (b c) -> p b c", b=blocks)

        tp_hi, tp_lo = in_arena(0, 2, PIXELS), in_arena(2, 2, PIXELS)
        pt_hi, pt_lo = in_arena(4, QBLOCKS, QUARTER), in_arena(6, QBLOCKS, QUARTER)
        g_hi, g_lo = in_arena(8, QBLOCKS, P), in_arena(9, QBLOCKS, P)

        LOW, HIGH = 0, 1

        def stack_of(grp, band):
            at = (2 * ((grp - 1) % GROUPS) + band) * PADDED
            return arena[0:STACK_ROWS, at:at + PADDED]

        def stack_block(grp):
            return (GROUP_CHUNKS * grp + 2) % BLOCKS

        assert 2 * PADDED <= 4 * PIXELS
        assert 2 * GROUPS * PADDED <= 10 * PIXELS

        hidden_halves = hidden[:, :, :].rearrange("p q n -> p (q n)").rearrange("p (s n) -> p s n", s=2)
        softmax_rows = [probs[:, 0, :], probs[:, 1, :], hidden_halves[:, 0, :], hidden_halves[:, 1, :]]
        g_t = hidden_halves[:, 1, :]

        def stage(n, a):
            whole = isinstance(n, int) and n == 0
            return softmax_rows[a if whole else min(a, 2)]

        mid_raw = x1[:, 0:2, :].rearrange("p k n -> p (k n)").rearrange("p (g q m) -> p g q m", g=GROUPS, q=PAIRS)
        w_stack_raw = probs[0:STACK_ROWS, 1, 0:3 * GROUPS * HIDDEN].rearrange("p (g v d) -> p g v d", g=GROUPS, v=3)
        w_cross_raw = probs[:, 0, 0:GROUPS * P].rearrange("p (g m) -> p g m", g=GROUPS)
        wp_raw = x1[:, 2:4, :].rearrange("p k n -> p (k n)")[:, 0:3 * BLOCKS * P].rearrange(
            "p (w k o) -> p w k o", w=3, k=BLOCKS)
        ww_raw = x1[:, 3, PIXELS - BLOCKS * P:PIXELS].rearrange("p (k o) -> p k o", k=BLOCKS)

        ps = ctx.enter_context(nc.psum_tensor("ps", [P, 8, HALF], F32))
        BANK_T, BANK_CROSS, BANK_Y, BANK_DX = 4, 5, 6, 7

        CROSSES = 2 * (SLOTS - 1)
        CROSSED = ((1, slice(HIDDEN, P)), (2, slice(0, HIDDEN)))

        WB, GAMMA, BETA, MEAN, VAR = range(5)

        def y_bank(j):
            return BANK_Y + j % 2

        def z_bank(j, v):
            return y_bank(j + 1 - v)

        score_banks = [ps[:, 0:2, :], ps[:, 2:4, :]]

        def padded(t, k):
            return t[:, k, :].rearrange("p (h w) -> p h w", w=PITCH)

        padded_all = xp[:, :, :].rearrange("p k (h w) -> p k h w", w=PITCH)

        def shifted_in(image, chunk, half):
            dr, dc = SHIFTS[chunk // BLOCKS]
            r0 = 1 + dr + HALF_ROWS * half
            return image.rearrange("p (h w) -> p h w", w=PITCH)[:, r0:r0 + HALF_ROWS, 1 + dc:1 + dc + SIDE]

        def shifted(t, chunk, half):
            return shifted_in(t[:, chunk % BLOCKS, :], chunk, half)

        def inside(t, k):
            return padded(t, k)[:, 1:1 + SIDE, 1:1 + SIDE]

        w_mid_loaded = [sem(f"w_mid_loaded_{g}") for g in range(GROUPS)]
        columns_loaded = sem("columns_loaded")
        w_l0_loaded = sem("w_l0_loaded")
        w_cross_loaded = sem("w_cross_loaded")
        w_stack_loaded = sem("w_stack_loaded")
        w_l1_loaded = sem("w_l1_loaded")
        borders_zero = sem("borders_zero")
        ident_zero = sem("ident_zero")
        ident_ready = sem("ident_ready")
        w_mid_rounded = sem("w_mid_rounded")
        w_mid_split = sem("w_mid_split")
        w_cross_rounded = sem("w_cross_rounded")
        w_cross_split = sem("w_cross_split")
        w_stack_rounded = sem("w_stack_rounded")
        w_stack_split = sem("w_stack_split")
        wp_rounded = sem("wp_rounded")
        wp_split = sem("wp_split")
        bn_step = sem("bn_step")
        var_ready = sem("var_ready")
        std_ready = sem("std_ready")
        ww_scaled = sem("ww_scaled")
        ww_transposed = sem("ww_transposed")
        ww_rounded = sem("ww_rounded")
        ww_split = sem("ww_split")

        x_loaded = [sem(f"x_loaded_{a}") for a in range(BLOCKS)]
        xp_copied = sem("xp_copied")
        xp_rounded = sem("xp_rounded")
        xp_split_odd = sem("xp_split_odd")
        xp_split_even = sem("xp_split_even")
        stacked = [sem(f"stacked_{g}") for g in range(GROUPS)]
        hidden_summed = sem("hidden_summed")
        hidden_ready = sem("hidden_ready")
        cross_summed = sem("cross_summed")
        cross_copied = sem("cross_copied")
        cross_added = sem("cross_added")
        cross_ready = [sem("cross_ready_0"), sem("cross_ready_1")]
        dx_summed = sem("dx_summed")
        x1_ready = sem("x1_ready")
        x1_rounded = sem("x1_rounded")
        x1_split = sem("x1_split")
        projected = sem("projected")
        proj_biased = sem("proj_biased")
        tp_split = sem("tp_split")
        scored = sem("scored")
        max_found = sem("max_found")
        exp_done = sem("exp_done")
        inv_done = sem("inv_done")
        normalized = sem("normalized")
        transposed = sem("transposed")
        t_rounded = sem("t_rounded")
        t_split = sem("t_split")
        y_summed = sem("y_summed")
        y_rounded = sem("y_rounded")
        y_split = sem("y_split")
        z_summed = sem("z_summed")
        out_added = sem("out_added")
        stored = [sem("stored_0"), sem("stored_1")]

        TH, PH, G = 0, 1, 2
        PROJECTIONS = [(0, TH, 4), (0, PH, 5), (1, PH, 4), (0, G, 5), (1, G, 4), (1, TH, 6)]
        TP_ORDER = [p[:2] for p in PROJECTIONS if p[1] != G]

        def proj_step(half, w):
            return [p[:2] for p in PROJECTIONS].index((half, w))

        T_PER = 2 * (QBLOCKS + 1)

        block = ctx.enter_context(nc.Block())

        @block.sync
        def _(sp):
            def load_x(n, a):
                k = ARRIVAL[a]
                sp.dma_start(stage(n, a), x[n, k * P:(k + 1) * P, :]).then_inc(x_loaded[a], 16)

            def load_first_blocks(n):
                sp.wait_ge(transposed, (n - 1) * T_PER)
                load_x(n, 0)
                load_x(n, 1)

            def store_quarter(n, j):
                sp.wait_ge(out_added, n * 8 + 2 * j + 2)
                sp.dma_start(out[n, :, j * QUARTER:(j + 1) * QUARTER].rearrange("(k p) n -> p k n", p=P),
                             x1[:, :, j * QUARTER:(j + 1) * QUARTER]).then_inc(stored[j // 2], 16)

            def batch(n, has_next, has_second):
                if has_next:
                    sp.wait_ge(dx_summed, n * SLOTS + SLOTS)
                    load_x(n + 1, 2)
                    sp.wait_ge(xp_copied, (n + 1) * BLOCKS + 3)
                    load_x(n + 1, 3)
                for j in range(QUARTERS):
                    store_quarter(n, j)
                if has_second:
                    load_first_blocks(n + 2)

            def load_w_mid(grp):
                sp.dma_start(mid_raw[:, grp, :, :], w_mid[:, grp]).then_inc(w_mid_loaded[grp], 16)

            load_x(0, 0)
            load_w_mid(0)
            load_x(0, 1)
            sp.dma_start(columns[:, :], per_channel).then_inc(columns_loaded, 16)
            load_x(0, 2)
            load_x(0, 3)
            sp.dma_start(w_ends_sb[:, :, :], w_ends).then_inc(w_l0_loaded, 16)
            load_w_mid(1)
            sp.wait_ge(xp_copied, 2)
            sp.dma_start(w_cross_raw, w_crosses).then_inc(w_cross_loaded, 16)
            sp.dma_start(w_stack_raw, w_stacks).then_inc(w_stack_loaded, 16)
            load_w_mid(2)
            load_w_mid(3)
            sp.dma_start(w2s[:, :, :], w2_pairs).then_inc(w_l0_loaded, 16)
            for w in range(3):
                sp.dma_start(wp_raw[:, w, :, :], proj_t[w].rearrange("(k p) o -> p k o", p=P)).then_inc(w_l1_loaded, 16)
            sp.dma_start(ww_raw, ww.rearrange("(k p) o -> p k o", p=P)).then_inc(w_l1_loaded, 16)
            sp.wait_ge(w_cross_split, 1)
            sp.wait_ge(w_stack_split, 1)
            load_x(1, 0)
            load_x(1, 1)

            with sp.Fori(0, BATCH - 2) as n:
                batch(n, True, True)
            batch(BATCH - 2, True, False)
            batch(BATCH - 1, False, False)
            for s in stored:
                sp.wait_ge(s, 16 * 2 * BATCH)

        W_L0_DMAS, W_L1_DMAS = 2, 4

        @block.tensor
        def _(pe):
            mm = nc.tensor.matmul

            def w_end(which, grp, q):
                return w_ends_sb[:, ENDS.index((which, grp, q)), :]

            def hidden_mid(n, s, q):
                half, grp = divmod(s, GROUPS)
                chunk = GROUP_CHUNKS * grp + 2 * q + 1
                if s > 0:
                    pe.wait_ge(hidden_ready, (n * SLOTS + s - 1) * PAIRS + pair_order(s - 1).index(q) + 1)
                    if s > 1 and q in (1, 2):
                        pe.wait_ge(cross_added, n * CROSSES + 2 * (s - 2) + q)
                elif q < 2:
                    pe.wait_ge(xp_split_odd, n * BY_VECTOR + q + 1)
                if s == 1 and q == pair_order(0)[0]:
                    pe.wait_ge(xp_split_even, (n + 1) * (BLOCKS - BY_VECTOR))
                mid_hi, mid_lo = w_mid_hi[:, grp, q, :], w_mid_lo[:, grp, q, :]
                for i, (w, image) in enumerate(((mid_hi, xp_hi), (mid_hi, xp_lo), (mid_lo, xp_hi))):
                    mm(ps[:, q, :], w, shifted(image, chunk, half), start=(i == 0), stop=False, skip_group_check=True)

            def hidden_ends(n, s, q):
                half, grp = divmod(s, GROUPS)
                chunk = GROUP_CHUNKS * grp + 2 * q
                if s == 0 and q == 0:
                    pe.wait_ge(xp_copied, (n + 1) * BLOCKS)
                mm(ps[0:HIDDEN, q, :], w_end(FIRST, grp, q), shifted(xp, chunk, half), start=False, stop=True,
                   skip_group_check=True)
                mm(ps[HIDDEN:P, q, :], w_end(LAST, grp, q), shifted(xp, chunk + 2, half), start=False, stop=True,
                   skip_group_check=True).then_inc(hidden_summed, 1)

            def hidden_cross(n, s):
                half, grp = divmod(s, GROUPS)
                if isinstance(n, int) and n == 0 and s == 1:
                    pe.wait_ge(w_cross_split, 1)
                if s > 1:
                    pe.wait_ge(cross_added, n * CROSSES + 2 * (s - 1))
                for i, (w, image) in enumerate(((w_cross_hi, xp_hi), (w_cross_hi, xp_lo), (w_cross_lo, xp_hi))):
                    last = mm(ps[:, BANK_CROSS, :], w[:, grp, :], shifted(image, GROUP_CHUNKS * grp + 4, half),
                              start=(i == 0), stop=(i == 2))
                last.then_inc(cross_summed, 1)

            def hidden_stacked(n, s):
                half, grp = divmod(s, GROUPS)
                if isinstance(n, int) and n == 0 and s == 1:
                    pe.wait_ge(w_stack_split, 1)
                if s <= GROUPS:
                    pe.wait_ge(stacked[grp], (n + 1) * 6 * 16)
                w = w_stack[:, grp, :, :].rearrange("p v d -> p (v d)")
                for q, band, chunk, w_cols in ((0, LOW, 2, w[:, HIDDEN:3 * HIDDEN]), (3, HIGH, 6, w[:, 0:2 * HIDDEN])):
                    mm(ps[:, q, :], w_cols, shifted_in(stack_of(grp, band), GROUP_CHUNKS * grp + chunk, half),
                       start=False, stop=False, skip_group_check=True)

            def hidden_outer(n, s):
                half, grp = divmod(s, GROUPS)
                chunk = GROUP_CHUNKS * grp
                mm(ps[0:HIDDEN, 0, :], w_end(FIRST, grp, 0), shifted(xp, chunk, half), start=False, stop=True,
                   skip_group_check=True).then_inc(hidden_summed, 1)
                mm(ps[HIDDEN:P, 3, :], w_end(LAST, grp, 3), shifted(xp, chunk + GROUP_CHUNKS - 1, half),
                   start=False, stop=True, skip_group_check=True).then_inc(hidden_summed, 1)

            def hidden_inner(n, s):
                half, grp = divmod(s, GROUPS)
                chunk = GROUP_CHUNKS * grp
                mm(ps[0:HIDDEN, 1, :], w_end(FIRST, grp, 1), shifted(xp, chunk + 2, half), start=False, stop=True,
                   skip_group_check=True).then_inc(hidden_summed, 1)
                mm(ps[HIDDEN:P, 2, :], w_end(LAST, grp, 2), shifted(xp, chunk + 6, half), start=False, stop=True,
                   skip_group_check=True).then_inc(hidden_summed, 1)

            def dx(n, s):
                pe.wait_ge(hidden_ready, n * SLOTS * PAIRS + (s + 1) * PAIRS)
                if s > 0:
                    for ready in cross_ready:
                        pe.wait_ge(ready, n * (SLOTS - 1) + s)
                if s > 0:
                    pe.wait_ge(x1_ready, n * SLOTS + s)
                elif not (isinstance(n, int) and n == 0):
                    pe.wait_ge(out_added, n * 8)
                for q in range(PAIRS):
                    last = mm(ps[32 * q:32 * q + 32, BANK_DX, :], w2s[:, (s % GROUPS) * PAIRS + q, :],
                              hidden[:, q, :], start=True, stop=True)
                last.then_inc(dx_summed, 1)

            def project(n, half, w):
                step = proj_step(half, w)
                bank = ps[:, PROJECTIONS[step][2], :]
                if step in (0, 2):
                    pe.wait_ge(x1_split, n * SLOTS + GROUPS * (half + 1))
                if 2 <= step < 5:
                    pe.wait_ge(tp_split, n * 4 + step - 1)
                cols = slice(half * HALF, (half + 1) * HALF)
                for k in range(BLOCKS):
                    mm(bank, wp_hi[:, w, k, :], x1_hi[:, k, cols], start=(k == 0), stop=False)
                    mm(bank, wp_hi[:, w, k, :], x1_lo[:, k, cols], start=False, stop=False)
                    last = mm(bank, wp_lo[:, w, k, :], x1_hi[:, k, cols], start=False, stop=(k == BLOCKS - 1))
                last.then_inc(projected, 1)

            def scores(n, i):
                if i == 0:
                    pe.wait_ge(tp_split, n * 4 + 3)
                if i == QBLOCKS // 2:
                    pe.wait_ge(tp_split, n * 4 + 4)
                if i >= 2:
                    pe.wait_ge(exp_done, n * QBLOCKS + i - 1)
                rows = slice(i * P, (i + 1) * P)
                for half in range(2):
                    bank, cols = ps[:, 2 * (i % 2) + half, :], slice(half * HALF, (half + 1) * HALF)
                    mm(bank, tp_hi[:, TH, rows], tp_hi[:, PH, cols], start=True, stop=False)
                    mm(bank, tp_hi[:, TH, rows], tp_lo[:, PH, cols], start=False, stop=False)
                    last = mm(bank, tp_lo[:, TH, rows], tp_hi[:, PH, cols], start=False, stop=True)
                last.then_inc(scored, 1)

            def transpose(n, tau):
                for u in range(2):
                    if tau == 0:
                        src = g_t
                        if u == 0:
                            pe.wait_ge(proj_biased, n * 6 + 5)
                    else:
                        if u == 0:
                            pe.wait_ge(normalized, n * QBLOCKS + tau)
                        pe.wait_ge(t_split, n * T_PER + 2 * (tau - 1) + u + 1)
                        src = softmax_rows[(tau - 1) % ROWS_HELD]
                    for v in range(4):
                        c = (4 * u + v) * P
                        last = nc.tensor.transpose(ps[:, BANK_T + u, v * P:(v + 1) * P], src[:, c:c + P], ident[:, :])
                    last.then_inc(transposed, 1)

            def attend(n, j):
                if j > 0:
                    pe.wait_ge(out_added, n * 8 + 2 * j - 1)
                bank = ps[:, y_bank(j), 0:QUARTER]
                for m in range(QBLOCKS):
                    if m % 4 == 0:
                        pe.wait_ge(t_split, n * T_PER + 2 * (2 * j + 2) + m // 4 + 1)
                    mm(bank, g_hi[:, m, :], pt_hi[:, m, :], start=(m == 0), stop=False)
                    mm(bank, g_hi[:, m, :], pt_lo[:, m, :], start=False, stop=False)
                    last = mm(bank, g_lo[:, m, :], pt_hi[:, m, :], start=False, stop=(m == QBLOCKS - 1))
                last.then_inc(y_summed, 1)

            def output(n, j, v):
                if v == 0:
                    pe.wait_ge(y_rounded, n * QUARTERS + j + 1)
                    if j > 0:
                        pe.wait_ge(out_added, n * 8 + 2 * j)
                places = [ps[:, z_bank(j, v), e * QUARTER:(e + 1) * QUARTER] for e in range(2)]
                for e in range(2):
                    c = slice((2 * v + e) * P, (2 * v + e + 1) * P)
                    mm(places[e], ww_hi[:, c], y_hi[:, :], start=(e == 0), stop=False, skip_group_check=True)
                    mm(places[e], ww_lo[:, c], y_hi[:, :], start=False, stop=False, skip_group_check=True)
                if v == 0:
                    pe.wait_ge(y_split, n * QUARTERS + j + 1)
                for e in range(2):
                    c = slice((2 * v + e) * P, (2 * v + e + 1) * P)
                    last = mm(places[e], ww_hi[:, c], y_lo[:, :], start=False, stop=True, skip_group_check=True)
                last.then_inc(z_summed, 1)

            def image_slot(n, s):
                for q in pair_order(s - 1):
                    hidden_mid(n, s, q)
                hidden_cross(n, s)
                hidden_stacked(n, s)
                dx(n, s - 1)
                hidden_outer(n, s)
                hidden_inner(n, s)

            def batch(n, has_next):
                project(n, 0, TH)
                dx(n, SLOTS - 1)
                project(n, 0, PH)
                project(n, 1, PH)
                project(n, 0, G)
                project(n, 1, G)
                scores(n, 0)
                transpose(n, 0)
                scores(n, 1)
                project(n, 1, TH)
                for i in range(QBLOCKS):
                    j = i // 2
                    if i % 2 == 0:
                        if i + 2 < QBLOCKS:
                            scores(n, i + 2)
                        elif has_next:
                            hidden_mid(n + 1, 0, 0)
                            hidden_mid(n + 1, 0, 1)
                        if j > 0:
                            attend(n, j - 1)
                        transpose(n, i + 1)
                    else:
                        if j > 0:
                            output(n, j - 1, 0)
                        if i + 2 < QBLOCKS:
                            scores(n, i + 2)
                        elif has_next:
                            hidden_mid(n + 1, 0, 2)
                            hidden_mid(n + 1, 0, 3)
                        transpose(n, i + 1)
                        if j > 0:
                            output(n, j - 1, 1)
                if has_next:
                    hidden_ends(n + 1, 0, 0)
                    hidden_ends(n + 1, 0, 1)
                attend(n, QUARTERS - 1)
                if has_next:
                    hidden_ends(n + 1, 0, 2)
                    hidden_ends(n + 1, 0, 3)
                output(n, QUARTERS - 1, 0)
                output(n, QUARTERS - 1, 1)
                if has_next:
                    for s in range(1, SLOTS):
                        image_slot(n + 1, s)

            pe.wait_ge(w_mid_split, 1)
            for q in range(PAIRS):
                hidden_mid(0, 0, q)
            pe.wait_ge(w_l0_loaded, 16 * W_L0_DMAS)
            for q in range(PAIRS):
                hidden_ends(0, 0, q)
            for s in range(1, GROUPS):
                pe.wait_ge(w_mid_split, s + 1)
                image_slot(0, s)
            pe.wait_ge(ident_ready, 1)
            pe.wait_ge(ww_scaled, BLOCKS)
            for k in range(BLOCKS):
                last = nc.tensor.transpose(ps[:, BANK_Y, k * P:(k + 1) * P], ww_raw[:, k, :], ident[:, :])
            last.then_inc(ww_transposed, 1)
            for s in range(GROUPS, SLOTS):
                image_slot(0, s)
            pe.wait_ge(wp_split, 1)
            pe.wait_ge(ww_split, 1)
            with pe.Fori(0, BATCH - 1) as n:
                batch(n, True)
            batch(BATCH - 1, False)

        @block.scalar
        def _(act):
            activation = nc.scalar.activation

            def relu(n, s, q):
                act.wait_ge(hidden_summed, (n * SLOTS + s) * PAIRS + pair_order(s).index(q) + 1)
                if q == 0 and s > 0:
                    act.wait_ge(dx_summed, n * SLOTS + s)
                rows = slice(0, P) if s == 0 or q in (0, 3) else slice(0, HIDDEN) if q == 1 else slice(HIDDEN, P)
                column = (s % GROUPS) * PAIRS + q
                activation(hidden[rows, q, :], ps[rows, q, :], ACT.Relu,
                           bias=b1s[rows, column:column + 1]).then_inc(hidden_ready, 1)

            def relu_crossed(n, s):
                q, rows = CROSSED[1]
                act.wait_ge(cross_added, n * CROSSES + 2 * s)
                activation(hidden[rows, q, :], hidden[rows, q, :], ACT.Relu).then_inc(cross_ready[1], 1)

            def round_x1(n, s):
                half, grp = divmod(s, GROUPS)
                act.wait_ge(x1_ready, n * SLOTS + s + 1)
                cols = slice(half * HALF, (half + 1) * HALF)
                nc.scalar.copy(x1_hi[:, grp, cols], x1[:, grp, cols]).then_inc(x1_rounded, 1)

            def bias_projection(n, half, w):
                step = proj_step(half, w)
                act.wait_ge(projected, n * 6 + step + 1)
                cols = slice(half * HALF, (half + 1) * HALF)
                if w == G:
                    act.wait_ge(dx_summed, n * SLOTS + SLOTS)
                dst = g_t[:, cols] if w == G else tp_hi[:, w, cols]
                activation(dst, ps[:, PROJECTIONS[step][2], :], ACT.Identity,
                           bias=pbs[:, w:w + 1]).then_inc(proj_biased, 1)

            def exp_rows(n, i):
                act.wait_ge(max_found, n * QBLOCKS + i + 1)
                if i < 3:
                    act.wait_ge(xp_copied, last_x_copied(n, i))
                else:
                    act.wait_ge(transposed, n * T_PER + 2 * (i - ROWS_HELD) + 4)
                e = slice(i % ROWS_HELD, i % ROWS_HELD + 1)
                activation(softmax_rows[i % ROWS_HELD], score_banks[i % 2], ACT.Exp,
                           bias=neg_max[:, i % 2:i % 2 + 1], accum_out=row_sum[:, e]).then_inc(exp_done, 1)

            def last_x_copied(n, i):
                if isinstance(n, int) and n == BATCH - 1:
                    return BATCH * BLOCKS
                return (n + 1) * BLOCKS + (i + 1 if i < 2 else BLOCKS)

            def round_transposed(n, tau):
                for u in range(2):
                    act.wait_ge(transposed, n * T_PER + 2 * tau + u + 1)
                    src = ps[:, BANK_T + u, :].rearrange("p (m n) -> p m n", m=4)
                    if tau == 0:
                        dst = g_hi[:, 4 * u:4 * u + 4, :]
                    else:
                        if u == 0 and tau >= 3 and tau % 2 == 1:
                            act.wait_ge(y_summed, n * QUARTERS + (tau - 1) // 2)
                        c = (tau - 1) % 2 * P
                        dst = pt_hi[:, 4 * u:4 * u + 4, c:c + P]
                    nc.scalar.copy(dst, src).then_inc(t_rounded, 1)

            def round_y(n, j):
                act.wait_ge(y_summed, n * QUARTERS + j + 1)
                if j > 0:
                    act.wait_ge(z_summed, n * 8 + 2 * j)
                nc.scalar.copy(y_hi[:, :], ps[:, y_bank(j), 0:QUARTER]).then_inc(y_rounded, 1)

            def round_image(n, a):
                act.wait_ge(xp_copied, n * BLOCKS + a + 1)
                nc.scalar.copy(xp_hi[:, ARRIVAL[a], :], xp[:, ARRIVAL[a], :]).then_inc(xp_rounded, 1)

            def image_slot(n, s):
                order = pair_order(s)
                relu(n, s, order[0])
                relu(n, s, order[1])
                relu(n, s, order[2])
                relu(n, s, order[3])
                relu_crossed(n, s)
                round_x1(n, s - 1)

            def batch(n, has_next):
                bias_projection(n, 0, TH)
                round_x1(n, SLOTS - 1)
                bias_projection(n, 0, PH)
                if has_next:
                    round_image(n + 1, 0)
                bias_projection(n, 1, PH)
                if has_next:
                    round_image(n + 1, 1)
                bias_projection(n, 0, G)
                if has_next:
                    round_image(n + 1, 2)
                bias_projection(n, 1, G)
                round_transposed(n, 0)
                exp_rows(n, 0)
                exp_rows(n, 1)
                bias_projection(n, 1, TH)
                for i in range(QBLOCKS):
                    j = i // 2
                    if i % 2 == 0 and j > 0:
                        if i + 2 < QBLOCKS:
                            exp_rows(n, i + 2)
                        round_y(n, j - 1)
                        round_transposed(n, i + 1)
                    else:
                        round_transposed(n, i + 1)
                        if i + 2 < QBLOCKS:
                            exp_rows(n, i + 2)
                    if i == 6 and has_next:
                        round_image(n + 1, 3)
                if has_next:
                    relu(n + 1, 0, 0)
                    relu(n + 1, 0, 1)
                round_y(n, QUARTERS - 1)
                if has_next:
                    relu(n + 1, 0, 2)
                    relu(n + 1, 0, 3)
                    for s in range(1, SLOTS):
                        image_slot(n + 1, s)

            def round_w_mid(grp):
                act.wait_ge(w_mid_loaded[grp], 16)
                nc.scalar.copy(w_mid_hi[:, grp, :, :], mid_raw[:, grp, :, :]).then_inc(w_mid_rounded, 1)

            round_image(0, 0)
            round_w_mid(0)
            round_image(0, 1)
            act.wait_ge(var_ready, 1)
            nc.scalar.sqrt(bn_b[:, :], bn_a[:, :]).then_inc(std_ready, 1)
            nc.scalar.preload_act_table(ACT.Exp)
            round_w_mid(1)
            act.wait_ge(w_cross_loaded, 16)
            nc.scalar.copy(w_cross_hi[:, :, :], w_cross_raw).then_inc(w_cross_rounded, 1)
            for a in range(2, BLOCKS):
                round_image(0, a)
                round_w_mid(a)
            act.wait_ge(columns_loaded, 16)
            for q in range(PAIRS):
                relu(0, 0, q)
            act.wait_ge(w_stack_loaded, 16)
            nc.scalar.copy(w_stack[:, :, :, :], w_stack_raw).then_inc(w_stack_rounded, 1)
            image_slot(0, 1)
            act.wait_ge(w_l1_loaded, 16 * W_L1_DMAS)
            nc.scalar.copy(wp_hi[:, :, :, :], wp_raw).then_inc(wp_rounded, 1)
            for s in range(2, GROUPS):
                image_slot(0, s)
            act.wait_ge(ww_transposed, 1)
            nc.scalar.copy(ww_hi[:, :], ps[:, BANK_Y, :]).then_inc(ww_rounded, 1)
            for s in range(GROUPS, SLOTS):
                image_slot(0, s)
            with act.Fori(0, BATCH - 1) as n:
                batch(n, True)
            batch(BATCH - 1, False)

        @block.vector
        def _(dve):
            stt = nc.vector.scalar_tensor_tensor

            def sum_x1(n, s):
                half, grp = divmod(s, GROUPS)
                dve.wait_ge(dx_summed, n * SLOTS + s + 1)
                image = inside(xp, grp)[:, half * HALF_ROWS:(half + 1) * HALF_ROWS, :]
                stt(out=x1[:, grp, half * HALF:(half + 1) * HALF].rearrange("p (h w) -> p h w", w=SIDE),
                    in0=ps[:, BANK_DX, :].rearrange("p (h w) -> p h w", w=SIDE), scalar=b2s[:, grp:grp + 1],
                    in1=image, op0=ALU.add, op1=ALU.add).then_inc(x1_ready, 1)

            def relu_crossed(n, s):
                dve.wait_ge(cross_summed, n * (SLOTS - 1) + s)
                dve.wait_ge(dx_summed, n * SLOTS + s)
                for e, (q, rows) in enumerate(CROSSED):
                    step = n * CROSSES + 2 * (s - 1) + e + 1
                    place, column = hidden[rows, q, :], (s % GROUPS) * PAIRS + q
                    nc.vector.tensor_scalar(place, ps[rows, BANK_CROSS, :], b1s[rows, column:column + 1], None,
                                            ALU.add).then_inc(cross_copied, 1)
                    dve.wait_ge(cross_copied, step)
                    nc.vector.tensor_tensor(place, ps[rows, q, :], place, ALU.add).then_inc(cross_added, 1)
                    if e == 0:
                        dve.wait_ge(cross_added, step)
                        nc.vector.tensor_scalar(place, place, 0.0, None, ALU.max).then_inc(cross_ready[0], 1)

            def sum_slot(n, s):
                relu_crossed(n, s)
                sum_x1(n, s - 1)
                split_x1(n, s - 1)

            def split_x1(n, s):
                half, grp = divmod(s, GROUPS)
                cols = slice(half * HALF, (half + 1) * HALF)
                dve.wait_ge(x1_rounded, n * SLOTS + s + 1)
                nc.vector.tensor_tensor(x1_lo[:, grp, cols], x1[:, grp, cols], x1_hi[:, grp, cols].bitcast(F32),
                                        ALU.subtract).then_inc(x1_split, 1)

            def split_projection(n, half, w):
                step = proj_step(half, w)
                dve.wait_ge(proj_biased, n * 6 + step + 1)
                cols = slice(half * HALF, (half + 1) * HALF)
                stt(out=tp_lo[:, w, cols], in0=ps[:, PROJECTIONS[step][2], :], scalar=pbs[:, w:w + 1],
                    in1=tp_hi[:, w, cols].bitcast(F32), op0=ALU.add, op1=ALU.subtract).then_inc(tp_split, 1)

            def copy_image(n, a):
                dve.wait_ge(x_loaded[a], (n + 1) * 16)
                nc.vector.tensor_copy(inside(xp, ARRIVAL[a]), stage(n, a).rearrange("p (h w) -> p h w", w=SIDE)
                                      ).then_inc(xp_copied, 1)

            def split_image(n, a):
                k = ARRIVAL[a]
                dve.wait_ge(xp_rounded, n * BLOCKS + a + 1)
                nc.vector.tensor_tensor(xp_lo[:, k, :], xp[:, k, :], xp_hi[:, k, :].bitcast(F32),
                                        ALU.subtract).then_inc(xp_split_odd if a < BY_VECTOR else xp_split_even, 1)

            def find_max(n, i):
                dve.wait_ge(scored, n * QBLOCKS + i + 1)
                nc.vector.tensor_reduce(neg_max[:, i % 2:i % 2 + 1], score_banks[i % 2], op=ALU.max, axis=AX.XY,
                                        negate=True).then_inc(max_found, 1)

            def invert_sum(n, i):
                e = slice(i % ROWS_HELD, i % ROWS_HELD + 1)
                dve.wait_ge(exp_done, n * QBLOCKS + i + 1)
                nc.vector.reciprocal(row_inv[:, e], row_sum[:, e]).then_inc(inv_done, 1)

            def split_transposed(n, tau):
                for u in range(2):
                    dve.wait_ge(t_rounded, n * T_PER + 2 * tau + u + 1)
                    src = ps[:, BANK_T + u, :].rearrange("p (m n) -> p m n", m=4)
                    if tau == 0:
                        hi, lo = (t[:, 4 * u:4 * u + 4, :] for t in (g_hi, g_lo))
                    else:
                        c = (tau - 1) % 2 * P
                        hi, lo = (t[:, 4 * u:4 * u + 4, c:c + P] for t in (pt_hi, pt_lo))
                    nc.vector.tensor_tensor(lo, src, hi.bitcast(F32), ALU.subtract).then_inc(t_split, 1)

            def split_y(n, j):
                dve.wait_ge(y_rounded, n * QUARTERS + j + 1)
                nc.vector.tensor_tensor(y_lo[:, :], ps[:, y_bank(j), 0:QUARTER], y_hi[:, :].bitcast(F32),
                                        ALU.subtract).then_inc(y_split, 1)

            def add_out(n, j, v):
                dve.wait_ge(z_summed, n * 8 + 2 * j + v + 1)
                for e in range(2):
                    k = 2 * v + e
                    place = x1[:, k, j * QUARTER:(j + 1) * QUARTER]
                    last = stt(out=place, in0=ps[:, z_bank(j, v), e * QUARTER:(e + 1) * QUARTER],
                               scalar=shift[:, k:k + 1], in1=place, op0=ALU.add, op1=ALU.add)
                last.then_inc(out_added, 1)

            def batch(n, has_next):
                sum_x1(n, SLOTS - 1)
                split_projection(n, 0, TH)
                split_x1(n, SLOTS - 1)
                if has_next:
                    dve.wait_ge(hidden_summed, (n + 1) * SLOTS * PAIRS)
                    copy_image(n + 1, 0)
                split_projection(n, 0, PH)
                if has_next:
                    copy_image(n + 1, 1)
                    split_image(n + 1, 0)
                    copy_image(n + 1, 2)
                split_projection(n, 1, PH)
                if has_next:
                    split_image(n + 1, 1)
                find_max(n, 0)
                split_transposed(n, 0)
                invert_sum(n, 0)
                find_max(n, 1)
                if has_next:
                    copy_image(n + 1, 3)
                invert_sum(n, 1)
                split_projection(n, 1, TH)
                find_max(n, 2)
                split_transposed(n, 1)
                for i in range(1, QBLOCKS):
                    j = i // 2
                    if i + 1 < QBLOCKS:
                        invert_sum(n, i + 1)
                    if i % 2 == 1 and j > 0:
                        add_out(n, j - 1, 0)
                    if i + 2 < QBLOCKS:
                        find_max(n, i + 2)
                    if i % 2 == 0 and j > 0:
                        split_y(n, j - 1)
                    split_transposed(n, i + 1)
                    if i % 2 == 1 and j > 0:
                        add_out(n, j - 1, 1)
                split_y(n, QUARTERS - 1)
                add_out(n, QUARTERS - 1, 0)
                add_out(n, QUARTERS - 1, 1)
                if has_next:
                    dve.wait_ge(stored[0], (n + 1) * 32)
                    for s in range(1, GROUPS + 1):
                        sum_slot(n + 1, s)
                    dve.wait_ge(stored[1], (n + 1) * 32)
                    for s in range(GROUPS + 1, SLOTS):
                        sum_slot(n + 1, s)

            dve.wait_ge(borders_zero, 1)
            copy_image(0, 0)
            copy_image(0, 1)
            split_image(0, 0)

            def split_w_mid(grp):
                dve.wait_ge(w_mid_rounded, grp + 1)
                nc.vector.tensor_tensor(w_mid_lo[:, grp, :, :], mid_raw[:, grp, :, :],
                                        w_mid_hi[:, grp, :, :].bitcast(F32), ALU.subtract).then_inc(w_mid_split, 1)

            split_w_mid(0)
            dve.wait_ge(columns_loaded, 16)
            nc.vector.tensor_scalar(bn_a[:, :], bn[:, VAR, :], BN_EPS, None, ALU.add).then_inc(var_ready, 1)
            copy_image(0, 2)
            split_image(0, 1)
            copy_image(0, 3)
            split_w_mid(1)
            dve.wait_ge(w_cross_rounded, 1)
            nc.vector.tensor_tensor(w_cross_lo[:, :, :], w_cross_raw, w_cross_hi[:, :, :].bitcast(F32),
                                    ALU.subtract).then_inc(w_cross_split, 1)
            split_image(0, 2)
            split_w_mid(2)
            split_image(0, 3)
            split_w_mid(3)
            dve.wait_ge(w_stack_rounded, 1)
            middle = slice(BAND, 2 * BAND)
            nc.vector.tensor_tensor(w_stack[middle], w_stack_raw[middle], w_stack[middle].bitcast(F32),
                                    ALU.subtract).then_inc(w_stack_split, 1)
            steps = [0]

            def chain(instruction):
                steps[0] += 1
                instruction.then_inc(bn_step, 1)
                dve.wait_ge(bn_step, steps[0])

            tt, ts = nc.vector.tensor_tensor, nc.vector.tensor_scalar
            dve.wait_ge(std_ready, 1)
            chain(nc.vector.reciprocal(inv[:, :], bn_b[:, :]))
            chain(tt(bn_b[:, :], inv[:, :], inv[:, :], ALU.mult))
            chain(tt(bn_b[:, :], bn_b[:, :], bn_a[:, :], ALU.mult))
            chain(ts(bn_b[:, :], bn_b[:, :], -0.5, 1.5, ALU.mult, ALU.add))
            chain(tt(inv[:, :], inv[:, :], bn_b[:, :], ALU.mult))
            chain(tt(inv[:, :], inv[:, :], bn[:, GAMMA, :], ALU.mult))
            chain(tt(shift[:, :], bn[:, WB, :], bn[:, MEAN, :], ALU.subtract))
            chain(tt(shift[:, :], shift[:, :], inv[:, :], ALU.mult))
            chain(tt(shift[:, :], shift[:, :], bn[:, BETA, :], ALU.add))
            dve.wait_ge(w_l1_loaded, 16 * W_L1_DMAS)
            for k in range(BLOCKS):
                ts(ww_raw[:, k, :], ww_raw[:, k, :], inv[:, k:k + 1], None, ALU.mult).then_inc(ww_scaled, 1)
            sum_slot(0, 1)
            dve.wait_ge(wp_rounded, 1)
            tt(wp_lo[:, :, :, :], wp_raw, wp_hi[:, :, :, :].bitcast(F32), ALU.subtract).then_inc(wp_split, 1)
            for s in range(2, GROUPS):
                sum_slot(0, s)
            dve.wait_ge(ww_rounded, 1)
            tt(ww_lo[:, :], ps[:, BANK_Y, :], ww_hi[:, :].bitcast(F32), ALU.subtract).then_inc(ww_split, 1)
            for s in range(GROUPS, SLOTS):
                sum_slot(0, s)
            with dve.Fori(0, BATCH - 1) as n:
                batch(n, True)
            batch(BATCH - 1, False)

        @block.gpsimd
        def _(pool):
            def normalize(n, i):
                pool.wait_ge(inv_done, n * QBLOCKS + i + 1)
                rows, e = softmax_rows[i % ROWS_HELD], slice(i % ROWS_HELD, i % ROWS_HELD + 1)
                nc.gpsimd.tensor_tensor(rows, rows, row_inv[:, e].to_broadcast([P, PIXELS]),
                                        ALU.mult).then_inc(normalized, 1)

            def split_image(n, a):
                k = ARRIVAL[a]
                pool.wait_ge(xp_rounded, n * BLOCKS + a + 1)
                nc.gpsimd.tensor_tensor(xp_lo[:, k, :], xp[:, k, :], xp_hi[:, k, :].bitcast(F32),
                                        ALU.subtract).then_inc(xp_split_even, 1)

            def hold(c):
                nc.gpsimd.tensor_tensor(held[:, c:c + 1], ident[:, 0:1], ident[:, 0:1], ALU.mult)

            def stack(n, grp):
                k = stack_block(grp)
                a = ARRIVAL.index(k)
                if a < BY_VECTOR:
                    pool.wait_ge(xp_split_odd, n * BY_VECTOR + a + 1)
                else:
                    pool.wait_ge(xp_split_even, n * (BLOCKS - BY_VECTOR) + a - BY_VECTOR + 1)
                hold(grp)
                for band, rows in enumerate((slice(0, BAND), slice(P - BAND, P))):
                    for part, image in enumerate((xp_hi, xp_hi, xp_lo)):
                        pool.dma_start(stack_of(grp, band)[part * BAND:(part + 1) * BAND, :],
                                       image[rows, k, :]).then_inc(stacked[grp], 16)

            def batch(n, has_next):
                if has_next:
                    split_image(n + 1, 2)
                for i in range(QBLOCKS):
                    normalize(n, i)
                if has_next:
                    pool.wait_ge(scored, (n + 1) * QBLOCKS)
                    hold(GROUPS)
                    stack(n + 1, 1)
                    split_image(n + 1, 3)
                    pool.wait_ge(y_summed, (n + 1) * QUARTERS)
                    hold(GROUPS + 1)
                    for grp in (2, 3, 0):
                        stack(n + 1, grp)

            for edge in (padded_all[:, :, 0:PITCH:PITCH - 1, :], padded_all[:, :, 1:1 + SIDE, 0:PITCH:PITCH - 1]):
                last = nc.gpsimd.memset(edge, 0.0)
            last.then_inc(borders_zero, 1)
            nc.gpsimd.memset(ident[:, :], 0.0).then_inc(ident_zero, 1)
            pool.wait_ge(ident_zero, 1)
            nc.gpsimd.affine_select(out=ident[:, :], in_=ident[:, :], compare_op=ALU.not_equal, fill=1.0, base=0,
                                    pattern=[[-1, P]], channel_multiplier=1).then_inc(ident_ready, 1)
            pool.wait_ge(ident_ready, 1)
            for grp in (1, 2, 3, 0):
                stack(0, grp)
            with pool.Fori(0, BATCH - 1) as n:
                batch(n, True)
            batch(BATCH - 1, False)


def kernel(x, L0_conv_w1, L0_conv_b1, L0_conv_w2, L0_conv_b2, L1_conv_theta_w, L1_conv_theta_b, L1_conv_phi_w,
           L1_conv_phi_b, L1_conv_g_w, L1_conv_g_b, L1_conv_w_w, L1_conv_w_b, L1_conv_bn_gamma, L1_conv_bn_beta,
           L1_conv_bn_mean, L1_conv_bn_var):
    import numpy as np
    import concourse.bacc as bacc
    from concourse.bass_utils import run_bass_kernel_spmd

    x = np.asarray(x)
    chunks = np.asarray(L0_conv_w1).transpose(0, 2, 1).reshape(GROUPS, GROUP_CHUNKS, P, HIDDEN).transpose(2, 0, 1, 3)
    w_mid = np.zeros((P, GROUPS, PAIRS, P), chunks.dtype)
    w_firsts_lasts = np.zeros((P, 2, GROUPS, PAIRS, HIDDEN), chunks.dtype)
    for q in range(PAIRS):
        begin, cut, end = BAND * q, BAND * q + BAND // 2, BAND * (q + 1)
        w_firsts_lasts[begin:, FIRST, :, q] = chunks[begin:, :, 2 * q]
        w_mid[:cut, :, q, :HIDDEN] = chunks[:cut, :, 2 * q + 1]
        w_mid[cut:, :, q, HIDDEN:] = chunks[cut:, :, 2 * q + 1]
        w_firsts_lasts[:end, LAST, :, q] = chunks[:end, :, 2 * q + 2]
    w_ends = np.stack([w_firsts_lasts[:, which, grp, q] for which, grp, q in ENDS], axis=1)
    w_crosses = np.zeros((P, GROUPS, P), chunks.dtype)
    w_crosses[P // 2:, :, :HIDDEN] = chunks[P // 2:, :, 4]
    w_crosses[:P // 2, :, HIDDEN:] = chunks[:P // 2, :, 4]
    w_stacks = np.zeros((3, BAND, GROUPS, 3, HIDDEN), chunks.dtype)
    w_stacks[:, :, :, 0] = chunks[P - BAND:, :, 6]
    w_stacks[:, :, :, 2] = chunks[:BAND, :, 2]
    w2 = np.asarray(L0_conv_w2).transpose(0, 2, 1).reshape(MODELS // 2, 2, HIDDEN, MODEL_CH)
    w2_pairs = np.zeros((2, HIDDEN, MODELS // 2, 2, MODEL_CH), w2.dtype)
    for model in range(2):
        w2_pairs[model, :, :, model] = w2[:, model].transpose(1, 0, 2)
    arrays = {
        "x": x.reshape(BATCH, CHANNELS, PIXELS),
        "w_mid": w_mid,
        "w_ends": w_ends,
        "w_crosses": w_crosses,
        "w_stacks": w_stacks.reshape(STACK_ROWS, GROUPS, 3, HIDDEN),
        "w2_pairs": w2_pairs.reshape(P, MODELS // 2, 2 * MODEL_CH),
        "proj_t": np.stack([np.asarray(w).T for w in (L1_conv_theta_w, L1_conv_phi_w, L1_conv_g_w)]),
        "ww": np.asarray(L1_conv_w_w),
        "per_channel": np.concatenate([np.asarray(v).reshape(-1, P) for v in (
            L0_conv_b1, L0_conv_b2, L1_conv_theta_b, L1_conv_phi_b, L1_conv_g_b, L1_conv_w_b, L1_conv_bn_gamma,
            L1_conv_bn_beta, L1_conv_bn_mean, L1_conv_bn_var)]).T,
    }
    arrays = {name: np.ascontiguousarray(a) for name, a in arrays.items()}
    nc = bacc.Bacc("TRN2", target_bir_lowering=False, num_devices=1)
    aps = {name: nc.dram_tensor(f"in_{name}", a.shape, mybir.dt.from_np(a.dtype), kind="ExternalInput").ap()
           for name, a in arrays.items()}
    out = nc.dram_tensor("out", (BATCH, CHANNELS, PIXELS), F32, kind="ExternalOutput").ap()
    conv_attention(nc, out=out, **aps)
    r = run_bass_kernel_spmd(nc, [{f"in_{name}": a for name, a in arrays.items()}], core_ids=[0])
    return r.results[0]["out"].reshape(x.shape)
```
